# Optimizing a Trainium2 kernel written in Bass

```python
import numpy as np
import jax
import jax.numpy as jnp

def _softmax(x, axis=-1):
    return jax.nn.softmax(x, axis=axis)

def _gelu(x):
    return jax.nn.gelu(x, approximate=True)

def _silu(x):
    return jax.nn.silu(x)

def _sigmoid(x):
    return jax.nn.sigmoid(x)

def _layernorm(x, axis=-1, eps=1e-05):
    m = jnp.mean(x, axis=axis, keepdims=True)
    v = jnp.var(x, axis=axis, keepdims=True)
    return (x - m) / jnp.sqrt(v + eps)

def _scatter_add(tgt, idx, src, axis=0):
    return tgt.at[idx].add(src)

def _segment_sum(src, seg, n):
    return jax.ops.segment_sum(src, seg, n)
kernel_name = 'mk_cond_resid_d2_seqx_r2_c8b920'

def setup_inputs(seed: int=0):
    np.random.seed(seed)
    _w = jnp.asarray

    def _rec_inputs():
        import jax
        import jax.numpy as jnp
        _rk = jax.random.key(seed)
        x = 7.22e-05 + 1 * jax.random.normal(jax.random.fold_in(_rk, 1), (8, 512, 1024), jnp.float32)
        _lenS = 512 - jax.random.randint(jax.random.fold_in(_rk, 7), (8,), 0, max(1, 512 // 4) + 1, jnp.int32)
        _lenS2 = 512 - jax.random.randint(jax.random.fold_in(_rk, 8), (8,), 0, max(1, 512 // 4) + 1, jnp.int32)
        cond_2048 = jax.random.bernoulli(jax.random.fold_in(_rk, 11), 0.5063, (8, 1024)).astype(jnp.float32)
        return (x, cond_2048)
    x, cond_2048 = _rec_inputs()

    def _L0_cond_setup():
        import jax, jax.numpy as jnp
        import numpy as np
        NH = 8
        NEG = -1e+30
        key = jax.random.key(seed)
        k1, k2, k3, k4 = jax.random.split(key, 4)
        B, D, T = (4, 512, 1024)
        x = jax.random.normal(k1, (B, D, T), dtype=jnp.float32)
        mask = jax.random.randint(k2, (B, T), 0, 2).astype(jnp.float32)
        lim = float(np.sqrt(6.0 / (D + D)))
        Wq = jax.random.uniform(k3, (D, D), dtype=jnp.float32, minval=-lim, maxval=lim)
        Wo = jax.random.uniform(k4, (D, D), dtype=jnp.float32, minval=-lim, maxval=lim)
        return {'x': x, 'mask': mask, 'Wq': Wq, 'Wo': Wo}
    _L0_cond_all = _L0_cond_setup()
    _L0_cond_in = {k: v for k, v in _L0_cond_all.items() if k in ('Wq', 'Wo')}
    del _L0_cond_all

    def _L1_cond_setup():
        import jax, jax.numpy as jnp
        import numpy as np
        key = jax.random.key(seed)
        k1, k2 = jax.random.split(key)
        B, T, C, K = (4, 2048, 1024, 4)
        x = jax.random.normal(k1, (B, T, C), dtype=jnp.float32)
        w = jax.random.normal(k2, (K, 1, C), dtype=jnp.float32) * 0.1
        return {'x': x, 'w': w}
    _L1_cond_all = _L1_cond_setup()
    _L1_cond_in = {k: v for k, v in _L1_cond_all.items() if k in ()}
    del _L1_cond_all
    return {'x': x, 'cond_2048': cond_2048, 'L0_cond_Wq': _L0_cond_in['Wq'], 'L0_cond_Wo': _L0_cond_in['Wo']}

def reference(x, cond_2048, L0_cond_Wq, L0_cond_Wo):
    import jax
    import jax.numpy as jnp

    def _L0_cond_ref(x, mask, Wq, Wo):
        import jax, jax.numpy as jnp
        import numpy as np
        NH = 8
        NEG = -1e+30
        B, D, T = x.shape
        dk = D // NH
        scale = 1.0 / jnp.sqrt(jnp.asarray(dk, x.dtype))
        xt = jnp.transpose(x, (0, 2, 1))
        q = xt @ Wq.T
        qh = q.reshape(B, T, NH, dk).transpose(0, 2, 1, 3)
        scores = scale * jnp.einsum('bhqd,bhkd->bhqk', qh, qh)
        cmask = mask[:, None, None, :]
        rmask = mask[:, None, :, None]
        logits = (scores * cmask + (1.0 - cmask) * NEG) * rmask
        attn = jax.nn.softmax(logits, axis=-1)
        ctx = jnp.einsum('bhqk,bhkd->bhqd', attn, qh)
        ctx = ctx.transpose(0, 2, 1, 3).reshape(B, T, D)
        out = ctx @ Wo.T
        return jnp.transpose(out, (0, 2, 1))

    def _L1_cond_ref(x, w):
        import jax, jax.numpy as jnp
        import numpy as np
        K = w.shape[0]
        C = x.shape[-1]
        y = jax.lax.conv_general_dilated(x, w, window_strides=(1,), padding=[(K - 1, 0)], dimension_numbers=('NHC', 'HIO', 'NHC'), feature_group_count=C)
        return y
    x = x + _L0_cond_ref(x, cond_2048, L0_cond_Wq, L0_cond_Wo)
    x = x + _L1_cond_ref(x, cond_2048[:, None, :])
    return x

_drawn_inputs = setup_inputs


def setup_inputs(seed=0):
    import zlib

    import numpy as np

    out = dict(_drawn_inputs(seed))
    spreads = {}
    factors = {}
    for name, (base, spread) in spreads.items():
        noise = np.random.default_rng([zlib.crc32(name.encode()), seed]).standard_normal(out[name].shape)
        drawn = base * np.exp(spread * noise) if base else spread * noise
        out[name] = jnp.asarray(drawn.astype(out[name].dtype))
    for name, factor in factors.items():
        out[name] = (out[name] * factor).astype(out[name].dtype)
    return out
```

```python
from contextlib import ExitStack

import concourse.bass as bass
from concourse import mybir

F32, F32R, I32 = mybir.dt.float32, mybir.dt.float32r, mybir.dt.int32
ALU, ACT, AX = mybir.AluOpType, mybir.ActivationFunctionType, mybir.AxisListType

B, D, T, HEADS, TAPS = 8, 512, 1024, 8, 8
P = 128
DK = D // HEADS
DC = D // P
PAIRS = HEADS // 2
TT = T // P
SCALE = DK ** -0.5
NEG = -1e30
PACKED = 640
PAD = TAPS - 1
BANK = 512
S0, S1, X, O = 0, 1, 2, 3


class Memory:
    pass


class Plan:

    def __init__(self, cap):
        self.cap, self.nt, self.half = cap, cap // P, cap // 2
        short = cap < T
        self.n_ab = 4 if short else 2
        self.n_cd = 2 if short else 1
        self.n_hl = 2
        self.n_p = 2 if short else 1
        self.n_ps = 2 if short else 1
        self.n_raw = 2 if short else 1
        self.shares = not short
        self.use, self.count = {}, [0, 0, 0, 0]
        nt = self.nt
        for c in range(DC):
            self._add(("T", c), (S0, S1, X, S0)[c])
        self._add(("Q", 0), S1)
        self._add(("Q", 1), X)
        for i in range(nt):
            self._add(("V", i), i % 2)
            for m in range(2 * i, 2 * i + 2):
                self._add(("M", 0, m), X)
        self._add(("MT", 0), X)
        for p in range(PAIRS):
            for i in range(nt):
                for hh in range(2):
                    self._add(("S", p, i, hh), hh)
                if i == 0 and p < 2:
                    self._add(("Q", p + 2), X)
                if p and i == 1:
                    self._add(("DEN", p - 1), X)
                if p and i == 2:
                    self._add(("RB", p - 1), X)
                if p + 1 < PAIRS:
                    for m in self.max_tiles(i):
                        self._add(("M", p + 1, m), X)
                    if i == nt - 2:
                        self._add(("MT", p + 1), X)
            self._add(("O", p), O)
        self._add(("DEN", PAIRS - 1), X)
        self._add(("RB", PAIRS - 1), X)
        for i in range(nt):
            self._add(("W", i), i % 2)
        self._add(("MEAN",), X)
        self.adds = nt - 1 if self.n_p > 1 else nt

    def _add(self, key, slot):
        self.use[key] = (slot, self.count[slot])
        self.count[slot] += 1

    def max_tiles(self, i):
        n, steps = 2 * self.nt, self.nt - 1
        return range(n * i // steps, n * (i + 1) // steps) if i < steps else range(0)

    def slot(self, key):
        return self.use[key][0]

    def before(self, b, key):
        return b * self.count[self.use[key][0]] + self.use[key][1]

    def after(self, b, key):
        return self.before(b, key) + 1

    def taps(self, i):
        n, steps = TAPS - 1, self.nt - 1
        return range(n * (i - 1) // steps, n * i // steps) if i else range(0)

    def read(self, b, step):
        if step < 0:
            if isinstance(b, int) and b == 0:
                return 0
            return self.read(b, step + PAIRS * self.nt) - PAIRS * self.adds
        p, i = divmod(step, self.nt)
        return b * PAIRS * self.adds + p * self.adds + (max(i, 1) if self.n_p > 1 else i + 1)

    def ab_value(self, b, p):
        return 16 * 8 * (b * (PAIRS // self.n_ab) + p // self.n_ab + 1)

    def cd_value(self, b, p):
        return 16 * 6 * (b * (PAIRS // self.n_cd) + p // self.n_cd + 1)

    def max_value(self, b, p):
        return 16 * 2 * (b * (PAIRS // self.n_cd) + p // self.n_cd + 1)

    def out_value(self, b, i):
        per_batch = (self.nt + 2 - i % 2) // 2
        return 16 * (b * per_batch + i // 2 + 1)


def wait(eng, sem, value):
    if not isinstance(value, int) or value > 0:
        eng.wait_ge(sem, value)


def batches(eng, body):
    body(0)
    body(1)
    with eng.Fori(2, B - 1) as b:
        body(b)
    body(B - 1)


def has_before(b):
    return not isinstance(b, int) or b > 0


def has_after(b):
    return not isinstance(b, int) or b < B - 1


def f32(ap):
    return ap.bitcast(F32)


def setup(nc, m):
    with ExitStack() as ctx:
        def sb(name, shape, dt=F32):
            return ctx.enter_context(nc.sbuf_tensor(name, shape, dt))

        def sem(name):
            return ctx.enter_context(nc.semaphore(name))

        wq_t, wo_t, wq_e = (sb(n, [P, DC, D]) for n in ("wq_t", "wo_t", "wq_e"))
        before = sb("before", [P, P])
        token_f, batch_at = sb("token_f", [P, B, TT]), sb("batch_at", [P, B, TT])
        batch_i = sb("batch_i", [P, B, TT], I32)
        order_i, order_f = sb("order_i", [B, T], I32), sb("order_f", [B, T])
        tail = sb("tail", [B, T])
        tile_sums, tile_base = sb("tile_sums", [P, B]), sb("tile_base", [P, B, TT])
        rank, place, spare = (sb(n, [P, B, TT]) for n in ("rank", "place", "spare"))
        n_valid, n_valid_row = sb("n_valid", [P, B]), sb("n_valid_row", [B, 1])
        most = sb("most", [P, 1])
        row_i = sb("row_i", [P, B, TT], I32)

        mask_in, weights_in, stored = sem("mask_in"), sem("weights_in"), sem("stored")
        iotas, blank, shapes_ready = sem("iotas"), sem("blank"), sem("shapes_ready")
        sums_ready, counted, chain, indices = sem("sums_ready"), sem("counted"), sem("chain"), sem("indices")
        high, mean_full, mean_out = sem("weights_high"), sem("mean_full"), sem("mean_out")
        mask3 = m.mask[:].rearrange("p (b j) -> p b j", b=B)
        prefix, totals = m.psum[S0][:, 0, 0:B * TT], m.psum[S0][:, 1, 0:B * TT]
        valid_all, valid_col = m.psum[X][:, 0, 0:B], m.psum[X][0:B, 1, 0:2]
        block = ctx.enter_context(nc.Block())

        @block.sync
        def _(sp):
            sp.dma_start(m.mask[:], m.maskT).then_inc(mask_in, 16)
            for dst, w in ((wq_t, m.wqT), (wo_t, m.woT), (wq_e, m.wq)):
                sp.dma_start(dst[:], w.rearrange("(c p) n -> p c n", p=P)).then_inc(weights_in, 16)
            sp.wait_ge(indices, 3)
            sp.dma_start(m.row_of.rearrange("b p j -> p b j"), row_i[:]).then_inc(stored, 16)
            sp.dma_start(m.tail_rows, tail[:]).then_inc(stored, 16)
            sp.wait_ge(stored, 32)

        @block.gpsimd
        def _(pool):
            nc.gpsimd.iota(m.token[:], [[T, B], [P, TT]], base=0, channel_multiplier=1).then_inc(iotas, 1)
            nc.gpsimd.iota(batch_i[:], [[T, B], [0, TT]], base=0, channel_multiplier=0).then_inc(iotas, 1)
            nc.gpsimd.iota(order_i[:], [[1, T]], base=0, channel_multiplier=0).then_inc(iotas, 1)
            nc.gpsimd.memset(m.ones[:], 1.0).then_inc(blank, 1)
            nc.gpsimd.memset(m.ident[:], 0.0).then_inc(blank, 1)
            nc.gpsimd.memset(m.head_tile[:], 0.0).then_inc(blank, 1)
            pool.wait_ge(blank, 3)
            nc.gpsimd.affine_select(out=m.head_tile[:], in_=m.head_tile[:], compare_op=ALU.not_equal, fill=1.0,
                                    base=0, pattern=[[1, 2 * TT], [-1, 2 * TT]],
                                    channel_multiplier=0).then_inc(shapes_ready, 1)
            nc.gpsimd.affine_select(out=m.ident[:], in_=m.ident[:], compare_op=ALU.not_equal, fill=1.0, base=0,
                                    pattern=[[-1, P]], channel_multiplier=1).then_inc(shapes_ready, 1)
            nc.gpsimd.affine_select(out=before[:], in_=m.ones[:], compare_op=ALU.is_ge, fill=0.0, base=-1,
                                    pattern=[[1, P]], channel_multiplier=-1).then_inc(shapes_ready, 1)
            pool.wait_ge(indices, 1)
            for j in range(TT):
                scatter_tokens(nc, m, j)
            pool.wait_ge(m.scattered, 16 * TT)

        @block.tensor
        def _(pe):
            pe.wait_ge(mask_in, 16)
            pe.wait_ge(shapes_ready, 3)
            pe.wait_ge(sums_ready, 1)
            nc.tensor.matmul(prefix, before[:], m.mask[:], start=True, stop=True)
            nc.tensor.matmul(totals, m.ones[:], m.mask[:], start=True, stop=True)
            nc.tensor.matmul(valid_all, m.ones[:], tile_sums[:], start=True, stop=True)
            nc.tensor.matmul(valid_col, tile_sums[:], m.ones[:, 0:2], start=True, stop=True).then_inc(counted, 1)
            pe.wait_ge(weights_in, 48)
            for g in range(DC):
                for c in range(DC):
                    last = nc.tensor.matmul(m.psum[(S1, O)[g // 2]][:, g % 2, :], wq_e[:, c, g * P:(g + 1) * P],
                                            wo_t[:, c, :], start=c == 0, stop=c == DC - 1)
                last.then_inc(mean_full, 1)

        @block.scalar
        def _(act):
            act.wait_ge(weights_in, 48)
            nc.scalar.activation(m.wq_hi[:], wq_t[:], ACT.Copy).then_inc(high, 1)
            nc.scalar.activation(m.wo_hi[:], wo_t[:], ACT.Copy).then_inc(high, 1)
            for g in range(DC):
                act.wait_ge(mean_full, g + 1)
                nc.scalar.activation(m.w_mean[:, g, :], m.psum[(S1, O)[g // 2]][:, g % 2, :],
                                     ACT.Copy).then_inc(mean_out, 1)
            act.wait_ge(mean_out, DC)

        @block.vector
        def _(dve):
            done = [0]

            def link(ins):
                done[0] += 1
                ins.then_inc(chain, 1)
                dve.wait_ge(chain, done[0])

            dve.wait_ge(mask_in, 16)
            nc.vector.tensor_reduce(tile_sums[:], mask3, AX.X, ALU.add).then_inc(sums_ready, 1)
            nc.vector.tensor_scalar(m.last_tap[:], m.mask[:, (TAPS - 1) * TT:TAPS * TT], 1.0, None, ALU.add)
            dve.wait_ge(iotas, 3)
            nc.vector.tensor_copy(token_f[:], m.token[:])
            nc.vector.tensor_copy(batch_at[:], batch_i[:])
            nc.vector.tensor_copy(order_f[:], order_i[:])
            link(nc.vector.memset(tile_base[:], 0.0))
            dve.wait_ge(counted, 1)
            tot3 = totals.rearrange("p (b j) -> p b j", b=B)
            for j in range(1, TT):
                link(nc.vector.tensor_tensor(tile_base[:, :, j], tile_base[:, :, j - 1], tot3[:, :, j - 1], ALU.add))
            nc.vector.tensor_copy(n_valid[:], valid_all)
            nc.vector.tensor_copy(n_valid_row[:], valid_col[:, 0:1])
            link(nc.vector.tensor_tensor(rank[:], tile_base[:], prefix.rearrange("p (b j) -> p b j", b=B), ALU.add))
            link(nc.vector.tensor_tensor(spare[:], token_f[:], rank[:], ALU.subtract))
            for b in range(B):
                last = nc.vector.tensor_scalar(spare[:, b, :], spare[:, b, :], n_valid[:, b:b + 1], None, ALU.add)
            link(last)
            link(nc.vector.tensor_tensor(place[:], rank[:], batch_at[:], ALU.add))
            link(nc.vector.tensor_tensor(place[:], place[:], spare[:], ALU.subtract))
            link(nc.vector.tensor_tensor(place[:], place[:], mask3, ALU.mult))
            link(nc.vector.tensor_tensor(place[:], place[:], spare[:], ALU.add))
            nc.vector.tensor_copy(m.place_i[:], place[:]).then_inc(indices, 1)
            link(nc.vector.tensor_scalar(rank[:], rank[:], 1.0, None, ALU.add))
            link(nc.vector.tensor_tensor(rank[:], rank[:], mask3, ALU.mult))
            nc.vector.tensor_copy(row_i[:], rank[:]).then_inc(indices, 1)
            nc.vector.tensor_scalar(tail[:], order_f[:], n_valid_row[:], NEG, ALU.is_ge, ALU.mult).then_inc(indices, 1)
            for b in range(B):
                nc.vector.tensor_scalar(m.valid[:, b, :], token_f[:, 0, :], n_valid[:, b:b + 1], None, ALU.is_lt)
            link(nc.vector.tensor_reduce(most[:], n_valid[:], AX.X, ALU.max))
            nc.vector.tensor_copy(m.most_valid[:], most[:])
            dve.wait_ge(high, 2)
            nc.vector.tensor_tensor(m.wq_lo[:], wq_t[:], f32(m.wq_hi[:]), ALU.subtract)
            link(nc.vector.tensor_tensor(m.wo_lo[:], wo_t[:], f32(m.wo_hi[:]), ALU.subtract))


def scatter_tokens(nc, m, column):
    nc.gpsimd.indirect_dma_start(
        m.token_at, bass.IndirectOffsetOnAxis(ap=m.place_i[:, column // TT, column % TT:column % TT + 1], axis=0),
        m.token[:, column // TT, column % TT:column % TT + 1], None).then_inc(m.scattered, 16)


def path_memory(nc, m, plan):
    n = Memory()
    cap, nt = plan.cap, plan.nt
    with ExitStack() as ctx:
        def sb(name, shape, dt=F32):
            return ctx.enter_context(nc.sbuf_tensor(f"{name}_{cap}", shape, dt))

        n.packed_out = nc.dram_tensor(f"packed_out_{cap}", [1 + cap, D], F32, kind="Internal").ap()
        n.token_idx = sb("token_idx", [P, nt], I32)
        n.row_idx = sb("row_idx", [P, TT], I32)
        n.xg = sb("xg", [P, nt, D])
        n.xt_hi, n.xt_lo = sb("xt_hi", [P, DC, cap], F32R), sb("xt_lo", [P, DC, cap], F32R)
        n.q_hi, n.q_lo = sb("q_hi", [P, plan.n_hl, cap], F32R), sb("q_lo", [P, plan.n_hl, cap], F32R)
        n.ab = sb("ab", [P, plan.n_ab, 2, 2, cap], F32R)
        n.cd = sb("cd", [P, plan.n_cd, 2, 2, cap], F32R)
        n.prob = sb("prob", [P, plan.n_p, 2, cap])
        n.prob_sum = sb("prob_sum", [P, plan.n_ps, 2, cap])
        n.v = sb("v", [P, nt, D])
        n.neg_max = sb("neg_max", [P, 2, 2 * nt])
        n.max_row = sb("max_row", [2 * nt, 2, P], F32R)
        n.raw = sb("raw", [P, plan.n_raw, cap])
        n.recip = sb("recip", [P, P])
        n.den = sb("den", [2 * nt, P])
        n.out_st = sb("out_st", [P, 2, D])
        n.xbar = sb("xbar", [P, DC])
        n.x1 = sb("x1", [P, 2, PAD + D + 1])
        n.g = sb("g", [P, 2, D])
        n.y = n.g if plan.shares else sb("y", [P, 2, D])
        n.xm = n.out_st[:].rearrange("p a c -> p (a c)") if plan.shares else sb("xm", [P, T])[:]
        n.valid_now = sb("valid_now", [P, TT])
        n.head_tile_v = m.head_tile[:, 0:2 * nt, 0:2 * nt]
    return n


def halves(ap, plan):
    return ap.rearrange("p (a c) -> p a c", a=2)


CONV_PAIR = 2 * (TAPS + 1)
CONV_BATCH = CONV_PAIR * (TT // 2)


def tensor_program(nc, pe, m, r, plan):
    nt, cap, half = plan.nt, plan.cap, plan.half

    def claim(b, key):
        wait(pe, m.free[plan.slot(key)], plan.before(b, key))
        return m.psum[plan.slot(key)]

    def filled(ins, key):
        ins.then_inc(m.full[plan.slot(key)], 1)

    def project(b, p):
        q = claim(b, ("Q", p))
        for a in range(2):
            n = 0
            for w, xt in ((m.wq_hi, r.xt_hi), (m.wq_lo, r.xt_hi), (m.wq_hi, r.xt_lo)):
                for c in range(DC):
                    last = nc.tensor.matmul(q[:, a, 0:half], w[:, c, p * P:(p + 1) * P],
                                            xt[:, c, a * half:(a + 1) * half], start=n == 0, stop=n == 3 * DC - 1)
                    n += 1
        filled(last, ("Q", p))

    def maxima(b, p, tiles):
        ab = r.ab[:, p % plan.n_ab]
        for t in tiles:
            hh, i = divmod(t, nt)
            s = claim(b, ("M", p, t))
            for a in range(2):
                last = nc.tensor.matmul(s[:, a, 0:half], ab[:, hh, 0, i * P:(i + 1) * P],
                                        ab[:, hh, 1, a * half:(a + 1) * half], start=True, stop=True)
            filled(last, ("M", p, t))

    def max_transpose(b, p):
        key = ("MT", p)
        s = claim(b, key)
        filled(nc.tensor.transpose(s[0:2 * nt, 0, 0:P], r.neg_max[:, p % 2, :], m.ident[:]), key)

    def denominators(b, p):
        s = claim(b, ("DEN", p))
        for hh in range(2):
            pe.wait_ge(m.added[hh], (b * PAIRS + p + 1) * plan.adds)
        for t in range(2 * nt):
            hh, i = divmod(t, nt)
            last = nc.tensor.matmul(s[0:2 * nt, 0, 0:P], r.head_tile_v[:, t, :],
                                    r.prob_sum[:, p % plan.n_ps, hh, i * P:(i + 1) * P],
                                    start=t == 0, stop=t == 2 * nt - 1)
        filled(last, ("DEN", p))

    def spread(b, p):
        s = claim(b, ("RB", p)).rearrange("p a c -> p (a c)")
        pe.wait_ge(m.recips, b * PAIRS + p + 1)
        for i in range(nt):
            for hh in range(2):
                row = m.ident[:, hh * nt + i:hh * nt + i + 1].to_broadcast([P, DK])
                last = nc.tensor.matmul(s[hh * DK:(hh + 1) * DK, i * P:(i + 1) * P], row, r.recip[:],
                                        start=True, stop=True)
        filled(last, ("RB", p))

    def context(b, p, i):
        if i == 0:
            claim(b, ("O", p))
        for hh in range(2):
            pe.wait_ge(m.free[hh], plan.after(b, ("S", p, i, hh)))
        step = p * nt + i
        for a in range(2):
            for hh in range(2):
                last = nc.tensor.matmul(m.psum[O][hh * DK:(hh + 1) * DK, a, 0:half],
                                        r.v[:, i, (2 * p + hh) * DK:(2 * p + hh + 1) * DK],
                                        r.prob[:, step % plan.n_p, hh, a * half:(a + 1) * half],
                                        start=i == 0, stop=i == nt - 1)
        last.then_inc(m.full[O], 1)

    def body(b):
        pe.wait_ge(m.rows_masked, (b + 1) * nt)
        for c in range(DC):
            s = claim(b, ("T", c)).rearrange("p a c -> p (a c)")
            for i in range(nt):
                last = nc.tensor.transpose(s[:, i * P:(i + 1) * P], r.xg[:, i, c * P:(c + 1) * P], m.ident[:])
            filled(last, ("T", c))
        for c in range(DC):
            pe.wait_ge(m.free[plan.slot(("T", c))], plan.after(b, ("T", c)))
        project(b, 0)
        project(b, 1)
        for i in range(nt):
            v = claim(b, ("V", i))
            n = 0
            for xt, w in ((r.xt_hi, m.wq_hi), (r.xt_lo, m.wq_hi), (r.xt_hi, m.wq_lo)):
                for c in range(DC):
                    last = nc.tensor.matmul(v[:, 0, :], xt[:, c, i * P:(i + 1) * P], w[:, c, :],
                                            start=n == 0, stop=n == 3 * DC - 1)
                    n += 1
            filled(last, ("V", i))
            if i == 0:
                pe.wait_ge(m.ab_in[0], plan.ab_value(b, 0))
            maxima(b, 0, range(2 * i, 2 * i + 2))
        max_transpose(b, 0)
        previous = None
        for p in range(PAIRS):
            ab, cd = r.ab[:, p % plan.n_ab], r.cd[:, p % plan.n_cd]
            for i in range(nt):
                if i == 0:
                    pe.wait_ge(m.ab_in[p % plan.n_ab], plan.ab_value(b, p))
                    pe.wait_ge(m.cd_in[p % plan.n_cd], plan.cd_value(b, p))
                    pe.wait_ge(m.max_in[p % plan.n_cd], plan.max_value(b, p))
                for hh in range(2):
                    s = claim(b, ("S", p, i, hh))
                    for a in range(2):
                        cols = slice(a * half, (a + 1) * half)
                        nc.tensor.matmul(s[:, a, 0:half], ab[:, hh, 0, i * P:(i + 1) * P], ab[:, hh, 1, cols],
                                         start=True, stop=False)
                        last = nc.tensor.matmul(s[:, a, 0:half], cd[:, hh, 0, i * P:(i + 1) * P],
                                                cd[:, hh, 1, cols], start=False, stop=True)
                    filled(last, ("S", p, i, hh))
                if previous:
                    context(b, *previous)
                previous = (p, i)
                if i == 0 and p < 2:
                    project(b, p + 2)
                if p and i == 1:
                    denominators(b, p - 1)
                if p and i == 2:
                    spread(b, p - 1)
                if p + 1 < PAIRS:
                    if i == 0:
                        pe.wait_ge(m.ab_in[(p + 1) % plan.n_ab], plan.ab_value(b, p + 1))
                    maxima(b, p + 1, plan.max_tiles(i))
                    if i == nt - 2:
                        max_transpose(b, p + 1)
        context(b, *previous)
        denominators(b, PAIRS - 1)
        spread(b, PAIRS - 1)
        pe.wait_ge(m.ctx_split, (b + 1) * PAIRS)
        for i in range(nt):
            w = claim(b, ("W", i))
            n = 0
            for ct, wo in ((r.xt_hi, m.wo_hi), (r.xt_lo, m.wo_hi), (r.xt_hi, m.wo_lo)):
                for c in range(DC):
                    last = nc.tensor.matmul(w[:, 0, :], ct[:, c, i * P:(i + 1) * P], wo[:, c, :],
                                            start=n == 0, stop=n == 3 * DC - 1)
                    n += 1
            filled(last, ("W", i))
        s = claim(b, ("MEAN",))
        pe.wait_ge(m.channel_mean, (b + 1) * DC)
        for c in range(DC):
            last = nc.tensor.matmul(s[0:1, 0, :], r.xbar[:, c:c + 1], m.w_mean[:, c, :],
                                    start=c == 0, stop=c == DC - 1)
        filled(last, ("MEAN",))

    batches(pe, body)


def scalar_program(nc, act, m, r, plan):
    nt, cap, half = plan.nt, plan.cap, plan.half

    def ready(b, key):
        act.wait_ge(m.full[plan.slot(key)], plan.after(b, key))
        return m.psum[plan.slot(key)]

    def drained(ins, key):
        ins.then_inc(m.free[plan.slot(key)], 1)

    def mask_rows(b, i):
        if i == 0:
            act.wait_ge(m.rows_in, 16 * nt * (b + 1))
            act.wait_ge(m.valid_ready, b + 1)
        nc.scalar.activation(r.xg[:, i, :], r.xg[:, i, :], ACT.Copy,
                             scale=r.valid_now[:, i:i + 1]).then_inc(m.rows_masked, 1)

    def high_of_projection(b, p):
        s = ready(b, ("Q", p))
        if p >= plan.n_hl:
            act.wait_ge(m.ab_in[(p - plan.n_hl) % plan.n_ab], plan.ab_value(b, p - plan.n_hl))
            act.wait_ge(m.cd_in[(p - plan.n_hl) % plan.n_cd], plan.cd_value(b, p - plan.n_hl))
        elif has_before(b):
            old = p - plan.n_hl + PAIRS
            act.wait_ge(m.ab_in[old % plan.n_ab], plan.ab_value(b - 1, old))
            act.wait_ge(m.cd_in[old % plan.n_cd], plan.cd_value(b - 1, old))
        nc.scalar.activation(halves(r.q_hi[:, p % plan.n_hl, :], plan), s[:, :, 0:half],
                             ACT.Copy).then_inc(m.high, 1)

    def max_row(b, p):
        s = ready(b, ("MT", p))
        if p >= 2:
            act.wait_ge(m.max_in[(p - 2) % plan.n_cd], plan.max_value(b, p - 2))
        elif has_before(b):
            act.wait_ge(m.max_in[(p + 2) % plan.n_cd], plan.max_value(b - 1, p + 2))
        drained(nc.scalar.activation(r.max_row[:, p % 2, :], s[0:2 * nt, 0, 0:P], ACT.Copy), ("MT", p))

    def body(b):
        if not has_before(b):
            for i in range(nt):
                mask_rows(0, i)
        for c in range(DC):
            s = ready(b, ("T", c)).rearrange("p a c -> p (a c)")
            nc.scalar.activation(r.xt_hi[:, c, :], s[:, 0:cap], ACT.Copy).then_inc(m.high, 1)
        high_of_projection(b, 0)
        high_of_projection(b, 1)
        for i in range(nt):
            s = ready(b, ("V", i))
            drained(nc.scalar.activation(r.v[:, i, :], s[:, 0, :], ACT.Copy), ("V", i))
        max_row(b, 0)
        for p in range(PAIRS):
            for i in range(nt):
                step = p * nt + i
                for hh in range(2):
                    s = ready(b, ("S", p, i, hh))
                    wait(act, m.full[O], b * PAIRS * nt + step - plan.n_p + 1)
                    wait(act, m.added[hh], plan.read(b, step - plan.n_p))
                    drained(nc.scalar.activation(halves(r.prob[:, step % plan.n_p, hh, :], plan),
                                                 s[:, :, 0:half], ACT.Exp, scale=SCALE), ("S", p, i, hh))
                if i == 0 and p:
                    raw_context(b, p - 1)
                if i == 0 and p < 2:
                    high_of_projection(b, p + 2)
                if i == 2 and p:
                    high_of_context(b, p - 1)
                if i == 1:
                    channel_mean(b, p)
                if p == PAIRS - 1 and has_after(b):
                    mask_rows(b + 1, i)
                if i == nt - 2 and p + 1 < PAIRS:
                    max_row(b, p + 1)
        raw_context(b, PAIRS - 1)
        high_of_context(b, PAIRS - 1)
        for i in range(nt):
            s = ready(b, ("W", i))
            wait(act, m.out_stored[i % 2], plan.out_value(b, i) - 16)
            drained(nc.scalar.activation(r.out_st[:, i % 2, :], s[:, 0, :], ACT.Copy), ("W", i))
        s = ready(b, ("MEAN",))
        wait(act, m.out_stored[nt % 2], plan.out_value(b, nt) - 16)
        drained(nc.scalar.activation(r.out_st[0:1, nt % 2, :], s[0:1, 0, :], ACT.Copy), ("MEAN",))

    def raw_context(b, p):
        act.wait_ge(m.full[O], (b * PAIRS + p + 1) * nt)
        wait(act, m.ctx_split, b * PAIRS + p - plan.n_raw + 1)
        nc.scalar.activation(halves(r.raw[:, p % plan.n_raw, :], plan), m.psum[O][:, :, 0:half],
                             ACT.Copy).then_inc(m.free[O], 1)

    def high_of_context(b, p):
        act.wait_ge(m.free[X], plan.after(b, ("RB", p)))
        nc.scalar.activation(r.xt_hi[:, p, :], r.raw[:, p % plan.n_raw, :], ACT.Copy).then_inc(m.high, 1)

    def channel_mean(b, c):
        act.wait_ge(m.xm_in, 16 * (b * DC + c + 1))
        nc.scalar.activation(r.xm, r.xm, ACT.Copy, scale=1.0 / T,
                             accum_out=r.xbar[:, c:c + 1]).then_inc(m.channel_mean, 1)

    batches(act, body)


def vector_program(nc, dve, m, r, plan):
    nt, cap, half = plan.nt, plan.cap, plan.half

    def ready(b, key):
        dve.wait_ge(m.full[plan.slot(key)], plan.after(b, key))
        return m.psum[plan.slot(key)]

    def drained(ins, key):
        ins.then_inc(m.free[plan.slot(key)], 1)

    def low_of_projection(b, p):
        s = ready(b, ("Q", p))
        dve.wait_ge(m.high, b * (DC + 2 * PAIRS) + DC + p + 1)
        drained(nc.vector.tensor_tensor(halves(r.q_lo[:, p % plan.n_hl, :], plan), s[:, :, 0:half],
                                        halves(f32(r.q_hi[:, p % plan.n_hl, :]), plan), ALU.subtract), ("Q", p))

    def maxima(b, p, tiles):
        for t in tiles:
            s = ready(b, ("M", p, t))
            drained(nc.vector.tensor_reduce(r.neg_max[:, p % 2, t:t + 1], s[:, :, 0:half], AX.XY, ALU.max,
                                            negate=True), ("M", p, t))

    def reciprocals(b, p):
        s = ready(b, ("DEN", p))
        drained(nc.vector.tensor_scalar(r.den[:], s[0:2 * nt, 0, 0:P], 1e-30, None, ALU.max), ("DEN", p))
        dve.wait_ge(m.free[X], plan.after(b, ("DEN", p)))
        nc.vector.reciprocal(r.recip[0:2 * nt, :], r.den[:]).then_inc(m.recips, 1)

    def normalise(b, p):
        s = ready(b, ("RB", p)).rearrange("p a c -> p (a c)")
        dve.wait_ge(m.free[O], b * PAIRS + p + 1)
        raw = r.raw[:, p % plan.n_raw, :]
        drained(nc.vector.tensor_tensor(raw, raw, s[:, 0:cap], ALU.mult), ("RB", p))

    def low_of_context(b, p):
        dve.wait_ge(m.high, b * (DC + 2 * PAIRS) + DC + PAIRS + p + 1)
        nc.vector.tensor_tensor(r.xt_lo[:, p, :], r.raw[:, p % plan.n_raw, :], f32(r.xt_hi[:, p, :]),
                                ALU.subtract).then_inc(m.ctx_split, 1)

    def conv_start(c, k):
        base = c * CONV_BATCH + k * CONV_PAIR
        dve.wait_ge(m.x1_in, 32 * (c * (TT // 2) + k + 1))
        dve.wait_ge(m.g_in, 32 * (c * (TT // 2) + k + 1))
        wait(dve, m.y_stored, 16 * (c * (TT // 2) + k))
        for u in range(2):
            nc.vector.tensor_tensor(r.x1[:, u, PAD:PAD + D], r.x1[:, u, PAD:PAD + D], r.g[:, u, :],
                                    ALU.add).then_inc(m.conv, 1)
        for u in range(2):
            dve.wait_ge(m.conv, base + u + 1)
            nc.vector.tensor_scalar(r.y[:, u, :], r.x1[:, u, PAD:PAD + D], m.last_tap[:, 2 * k + u:2 * k + u + 1],
                                    None, ALU.mult).then_inc(m.conv, 1)

    def conv_taps(c, k, taps):
        base = c * CONV_BATCH + k * CONV_PAIR
        for tap in taps:
            for u in range(2):
                dve.wait_ge(m.conv, base + 2 * tap + 3 + u)
                j = tap * TT + 2 * k + u
                nc.vector.scalar_tensor_tensor(r.y[:, u, :], r.x1[:, u, tap:tap + D], m.mask[:, j:j + 1],
                                               r.y[:, u, :], ALU.mult, ALU.add).then_inc(m.conv, 1)

    def body(b):
        if isinstance(b, int) and b == 0:
            nc.vector.memset(r.x1[:], 0.0).then_inc(m.zeroed, 1)
            nc.vector.memset(r.recip[:], 0.0).then_inc(m.zeroed, 1)
            for n in range(plan.n_cd):
                for hh in range(2):
                    nc.vector.memset(f32(r.cd[DK:P, n, hh, 0, :]), 0.0).then_inc(m.zeroed, 1)
                    nc.vector.memset(f32(r.cd[DK:P, n, hh, 1, :]), 1.0).then_inc(m.zeroed, 1)
            dve.wait_ge(m.zeroed, 2 + 4 * plan.n_cd)
            for n in range(plan.n_cd):
                for hh in range(2):
                    nc.vector.memset(f32(r.cd[DK:DK + 1, n, hh, 0, :]), 1.0).then_inc(m.zeroed, 1)
            nc.vector.tensor_copy(r.valid_now[:], m.valid[:, 0, :]).then_inc(m.valid_ready, 1)
        for c in range(DC):
            s = ready(b, ("T", c)).rearrange("p a c -> p (a c)")
            dve.wait_ge(m.high, b * (DC + 2 * PAIRS) + c + 1)
            drained(nc.vector.tensor_tensor(r.xt_lo[:, c, :], s[:, 0:cap], f32(r.xt_hi[:, c, :]), ALU.subtract),
                    ("T", c))
        if has_after(b):
            nxt = m.valid[:, b + 1, :] if isinstance(b, int) else m.valid[:, bass.ds(b + 1, 1), :].rearrange("p o j -> p (o j)")
            nc.vector.tensor_copy(r.valid_now[:], nxt).then_inc(m.valid_ready, 1)
        low_of_projection(b, 0)
        low_of_projection(b, 1)
        for i in range(nt):
            maxima(b, 0, range(2 * i, 2 * i + 2))
        for p in range(PAIRS):
            for i in range(nt):
                if i == 0 and p < 2:
                    low_of_projection(b, p + 2)
                if p and i == 1:
                    reciprocals(b, p - 1)
                if p and i == 2:
                    normalise(b, p - 1)
                if p + 1 < PAIRS:
                    maxima(b, p + 1, plan.max_tiles(i))
                if p and i == 2:
                    low_of_context(b, p - 1)
                if p and has_before(b):
                    if i == 0:
                        conv_start(b - 1, p - 1)
                    conv_taps(b - 1, p - 1, plan.taps(i))
        reciprocals(b, PAIRS - 1)
        normalise(b, PAIRS - 1)
        low_of_context(b, PAIRS - 1)
        if has_before(b):
            conv_start(b - 1, PAIRS - 1)
            conv_taps(b - 1, PAIRS - 1, range(TAPS - 1))

    batches(dve, body)
    for k in range(TT // 2):
        conv_start(B - 1, k)
        conv_taps(B - 1, k, range(TAPS - 1))


def gpsimd_program(nc, pool, m, r, plan):
    nt = plan.nt

    def hold(sem, value):
        if not isinstance(value, int) or value > 0:
            pool.wait_ge(sem, value)
            pool.sem_inc(m.pool_passed, 1)

    def gather_rows(b):
        hold(m.tokens_in, 16 * (b + 1))
        if has_before(b):
            hold(m.full[plan.slot(("T", DC - 1))], plan.after(b - 1, ("T", DC - 1)))
        for i in range(nt):
            nc.gpsimd.indirect_dma_start(r.xg[:, i, :], None, m.xT,
                                         bass.IndirectOffsetOnAxis(ap=r.token_idx[:, i:i + 1], axis=0)
                                         ).then_inc(m.rows_in, 16)

    def gather_outputs(c, k):
        if k == 0:
            hold(m.out_rows_in, 16 * (c + 1))
            for i in (nt - 1, nt):
                hold(m.out_stored[i % 2], plan.out_value(c, i))
        hold(m.conv, c * CONV_BATCH + (CONV_PAIR * (k - 1) + 2 if k else 0))
        if plan.shares:
            hold(m.y_stored, 16 * (c * (TT // 2) + k))
        for u in range(2):
            nc.gpsimd.indirect_dma_start(r.g[:, u, :], None, r.packed_out,
                                         bass.IndirectOffsetOnAxis(ap=r.row_idx[:, 2 * k + u:2 * k + u + 1], axis=0)
                                         ).then_inc(m.g_in, 16)

    def body(b):
        if isinstance(b, int) and b == 0:
            gather_rows(0)
        for p in range(PAIRS):
            for i in range(nt):
                step = p * nt + i
                if i == 0:
                    if p >= plan.n_ps:
                        pool.wait_ge(m.full[X], plan.after(b, ("DEN", p - plan.n_ps)))
                    elif has_before(b):
                        pool.wait_ge(m.full[X], plan.after(b - 1, ("DEN", p - plan.n_ps + PAIRS)))
                for hh in range(2):
                    total = r.prob_sum[:, p % plan.n_ps, hh, :]
                    now = r.prob[:, step % plan.n_p, hh, :]
                    if i or plan.n_p == 1:
                        hold(m.free[hh], plan.after(b, ("S", p, i, hh)))
                    if i == 0:
                        if plan.n_p == 1:
                            nc.gpsimd.tensor_copy(total, now).then_inc(m.added[hh], 1)
                        continue
                    wait(pool, m.added[hh], plan.read(b, step) - 1)
                    first = r.prob[:, (step - 1) % plan.n_p, hh, :] if i == 1 and plan.n_p > 1 else total
                    nc.gpsimd.tensor_tensor(total, first, now, ALU.add).then_inc(m.added[hh], 1)
            if has_before(b):
                gather_outputs(b - 1, p)
            if isinstance(b, int) and b == 0:
                for column in range(TT, B * TT) if p == 0 else ():
                    scatter_tokens(nc, m, column)
            if p == 1 and has_after(b):
                gather_rows(b + 1)

    batches(pool, body)
    for k in range(TT // 2):
        gather_outputs(B - 1, k)


def sync_program(nc, sp, m, r, plan):
    nt, cap = plan.nt, plan.cap

    def hold(sem, value):
        if not isinstance(value, int) or value > 0:
            sp.wait_ge(sem, value)
            sp.sem_inc(m.sync_passed, 1)

    def tokens(b):
        if has_before(b):
            hold(m.scattered, 16 * B * TT)
            hold(m.rows_in, 16 * nt * b)
        sp.dma_start(r.token_idx[:], m.token_at3[b].rearrange("(j p) -> p j", p=P)[:, 0:nt],
                     allow_slow_non_contiguous=True).then_inc(m.tokens_in, 16)

    def first_operands(b, p):
        buf = p % plan.n_ab
        hold(m.free[plan.slot(("Q", p))], plan.after(b, ("Q", p)))
        if p >= plan.n_ab:
            hold(m.full[S1], plan.after(b, ("S", p - plan.n_ab, nt - 1, 1)))
        elif has_before(b):
            hold(m.full[S1], plan.after(b - 1, ("S", p - plan.n_ab + PAIRS, nt - 1, 1)))
        for hh in range(2):
            rows = slice(hh * DK, (hh + 1) * DK)
            hi, lo = f32(r.q_hi[rows, p % plan.n_hl, :]), f32(r.q_lo[rows, p % plan.n_hl, :])
            for lower, which, part in ((0, 0, hi), (1, 0, lo), (0, 1, hi), (1, 1, hi)):
                sp.dma_start(f32(r.ab[lower * DK:(lower + 1) * DK, buf, hh, which, :]), part
                             ).then_inc(m.ab_in[buf], 16)

    def second_operands(b, p):
        buf = p % plan.n_cd
        hold(m.free[plan.slot(("Q", p))], plan.after(b, ("Q", p)))
        if p >= plan.n_cd:
            hold(m.full[S1], plan.after(b, ("S", p - plan.n_cd, nt - 1, 1)))
        elif has_before(b):
            hold(m.full[S1], plan.after(b - 1, ("S", p - plan.n_cd + PAIRS, nt - 1, 1)))
        else:
            hold(m.zeroed, 2 + 6 * plan.n_cd)
        for hh in range(2):
            rows = slice(hh * DK, (hh + 1) * DK)
            sp.dma_start(f32(r.cd[0:DK, buf, hh, 0, :]), f32(r.q_hi[rows, p % plan.n_hl, :])
                         ).then_inc(m.cd_in[buf], 16)
            sp.dma_start(f32(r.cd[0:DK, buf, hh, 1, :]), f32(r.q_lo[rows, p % plan.n_hl, :])
                         ).then_inc(m.cd_in[buf], 16)
            sp.dma_start(f32(r.cd[DK + 1:DK + 2, buf, hh, 0, :]), m.tail_rows[bass.ds(b, 1), 0:cap]
                         ).then_inc(m.cd_in[buf], 16)

    def max_rows(b, p):
        buf = p % plan.n_cd
        hold(m.free[X], plan.after(b, ("MT", p)))
        for hh in range(2):
            sp.dma_start(f32(r.cd[DK:DK + 1, buf, hh, 1, :]).rearrange("o (i q) -> o i q", i=nt),
                         f32(r.max_row[hh * nt:(hh + 1) * nt, p % 2, :])).then_inc(m.max_in[buf], 16)

    def conv_load(c, k):
        hold(m.conv, c * CONV_BATCH + k * CONV_PAIR)
        if k == 0 and isinstance(c, int) and c == 0:
            hold(m.zeroed, 1)
        for u in range(2):
            sp.dma_start(r.x1[:, u, PAD:PAD + D], m.xT3[c * TT + 2 * k + u]).then_inc(m.x1_in, 16)

    def conv_store(c, k):
        hold(m.conv, c * CONV_BATCH + (k + 1) * CONV_PAIR)
        sp.dma_start(m.out4[c * (TT // 2) + k], r.y[:]).then_inc(m.y_stored, 16)

    def mean_load(b, c):
        if plan.shares and c == 0 and has_before(b):
            for i in (nt - 1, nt):
                hold(m.out_stored[i % 2], plan.out_value(b - 1, i))
        hold(m.channel_mean, b * DC + c)
        sp.dma_start(r.xm, m.x4[b * DC + c]).then_inc(m.xm_in, 16)

    def output_rows(c):
        hold(m.g_in, 32 * (TT // 2) * c)
        sp.dma_start(r.row_idx[:], m.row_of[c]).then_inc(m.out_rows_in, 16)

    def body(b):
        if isinstance(b, int) and b == 0:
            tokens(0)
        mean_load(b, 0)
        first_operands(b, 0)
        second_operands(b, 0)
        if has_before(b):
            output_rows(b - 1)
        first_operands(b, 1)
        if plan.n_cd > 1:
            second_operands(b, 1)
        max_rows(b, 0)
        for p in range(PAIRS):
            if p < 2:
                if p + 2 < plan.n_ab:
                    first_operands(b, p + 2)
            if p and p + 1 < PAIRS and plan.n_ab <= p + 1:
                first_operands(b, p + 1)
            if p and p + 1 < PAIRS and plan.n_cd > 1:
                second_operands(b, p + 1)
            if has_before(b) and p == 0:
                conv_load(b - 1, 0)
            if p + 1 < DC:
                mean_load(b, p + 1)
            if p == 0 and has_after(b):
                tokens(b + 1)
            if p + 1 < PAIRS:
                if plan.n_cd == 1:
                    second_operands(b, p + 1)
                max_rows(b, p + 1)
            if has_before(b) and p:
                conv_store(b - 1, p - 1)
                conv_load(b - 1, p)
        hold(m.g_in, 32 * (TT // 2) * b)
        for i in range(nt):
            hold(m.free[i % 2], plan.after(b, ("W", i)))
            sp.dma_start(r.packed_out[1 + i * P:1 + (i + 1) * P, :], r.out_st[:, i % 2, :]
                         ).then_inc(m.out_stored[i % 2], 16)
        hold(m.free[X], plan.after(b, ("MEAN",)))
        sp.dma_start(r.packed_out[0:1, :], r.out_st[0:1, nt % 2, :]
                     ).then_inc(m.out_stored[nt % 2], 16)
        if has_before(b):
            conv_store(b - 1, PAIRS - 1)

    batches(sp, body)
    output_rows(B - 1)
    for k in range(TT // 2):
        conv_load(B - 1, k)
        conv_store(B - 1, k)
    hold(m.y_stored, 16 * B * (TT // 2))


def cond_attn_conv(nc, xT, x, maskT, wqT, woT, wq, out):
    with ExitStack() as ctx:
        def sb(name, shape, dt=F32):
            return ctx.enter_context(nc.sbuf_tensor(name, shape, dt))

        def sem(name):
            return ctx.enter_context(nc.semaphore(name))

        def sems(name, n):
            return [sem(f"{name}{i}") for i in range(n)]

        m = Memory()
        m.xT, m.maskT, m.wqT, m.woT, m.wq = xT, maskT, wqT, woT, wq
        m.xT3 = xT.rearrange("(n p) d -> n p d", p=P)
        m.x4 = x.rearrange("(n p) t -> n p t", p=P)
        m.out4 = out.rearrange("(n u p) d -> n p u d", p=P, u=2)
        m.token_at = nc.dram_tensor("token_at", [B * T, 1], I32, kind="Internal").ap()
        m.token_at3 = m.token_at.rearrange("(b t) o -> b (t o)", b=B)
        m.row_of = nc.dram_tensor("row_of", [B, P, TT], I32, kind="Internal").ap()
        m.tail_rows = nc.dram_tensor("tail_rows", [B, T], F32, kind="Internal").ap()

        m.mask = sb("mask", [P, B * TT])
        m.wq_hi, m.wq_lo = sb("wq_hi", [P, DC, D], F32R), sb("wq_lo", [P, DC, D], F32R)
        m.wo_hi, m.wo_lo = sb("wo_hi", [P, DC, D], F32R), sb("wo_lo", [P, DC, D], F32R)
        m.w_mean = sb("w_mean", [P, DC, D])
        m.ident, m.ones = sb("ident", [P, P]), sb("ones", [P, P])
        m.head_tile = sb("head_tile", [P, 2 * TT, 2 * TT])
        m.valid = sb("valid", [P, B, TT])
        m.last_tap = sb("last_tap", [P, TT])
        m.place_i, m.token = sb("place_i", [P, B, TT], I32), sb("token", [P, B, TT], I32)
        m.most_valid = sb("most_valid", [P, 1], I32)
        m.psum = [ctx.enter_context(nc.psum_tensor(f"slot{n}", [P, 2, BANK], F32)) for n in range(4)]
        m.scattered, m.zeroed, m.valid_ready = sem("scattered"), sem("zeroed"), sem("valid_ready")
        m.recips, m.ctx_split, m.conv = sem("recips"), sem("ctx_split"), sem("conv")
        m.rows_masked, m.high, m.channel_mean = sem("rows_masked"), sem("high"), sem("channel_mean")
        m.sync_passed, m.pool_passed = sem("sync_passed"), sem("pool_passed")
        m.tokens_in, m.rows_in, m.xm_in = sem("tokens_in"), sem("rows_in"), sem("xm_in")
        m.out_rows_in, m.g_in, m.x1_in = sem("out_rows_in"), sem("g_in"), sem("x1_in")
        m.y_stored = sem("y_stored")
        m.full, m.free = sems("full", 4), sems("free", 4)
        m.added = sems("added", 2)
        m.ab_in, m.cd_in, m.max_in = sems("ab_in", 4), sems("cd_in", 2), sems("max_in", 2)
        m.out_stored = sems("out_stored", 2)

        setup(nc, m)
        short, full = ((path_memory(nc, m, plan), plan) for plan in (Plan(PACKED), Plan(T)))
        block = ctx.enter_context(nc.Block())

        @block.tensor
        def _(pe):
            fits = pe.value_load(m.most_valid[0:1, 0:1])
            with pe.If(fits < PACKED + 1):
                tensor_program(nc, pe, m, *short)
            with pe.Else():
                tensor_program(nc, pe, m, *full)

        @block.scalar
        def _(act):
            fits = act.value_load(m.most_valid[0:1, 0:1])
            with act.If(fits < PACKED + 1):
                scalar_program(nc, act, m, *short)
            with act.Else():
                scalar_program(nc, act, m, *full)

        @block.vector
        def _(dve):
            fits = dve.value_load(m.most_valid[0:1, 0:1])
            with dve.If(fits < PACKED + 1):
                vector_program(nc, dve, m, *short)
            with dve.Else():
                vector_program(nc, dve, m, *full)

        @block.gpsimd
        def _(pool):
            fits = pool.value_load(m.most_valid[0:1, 0:1])
            with pool.If(fits < PACKED + 1):
                gpsimd_program(nc, pool, m, *short)
            with pool.Else():
                gpsimd_program(nc, pool, m, *full)

        @block.sync
        def _(sp):
            fits = sp.value_load(m.most_valid[0:1, 0:1])
            with sp.If(fits < PACKED + 1):
                sync_program(nc, sp, m, *short)
            with sp.Else():
                sync_program(nc, sp, m, *full)


def kernel(x, cond_2048, L0_cond_Wq, L0_cond_Wo):
    import numpy as np
    import concourse.bacc as bacc
    from concourse.bass_utils import run_bass_kernel_spmd as run

    x, cond, wq, wo = (np.ascontiguousarray(a) for a in (x, cond_2048, L0_cond_Wq, L0_cond_Wo))
    arrays = {
        "xT": np.ascontiguousarray(x.transpose(0, 2, 1)).reshape(B * T, D),
        "x": x.reshape(B * D, T),
        "maskT": np.ascontiguousarray(cond.reshape(B * TT, P).T),
        "wqT": np.ascontiguousarray(wq.T),
        "woT": np.ascontiguousarray(wo.T),
        "wq": wq,
    }
    nc = bacc.Bacc("TRN2", target_bir_lowering=False, num_devices=1)
    args = [nc.dram_tensor(name, a.shape, F32, kind="ExternalInput").ap() for name, a in arrays.items()]
    out = nc.dram_tensor("out", [B * T, D], F32, kind="ExternalOutput").ap()
    cond_attn_conv(nc, *args, out)
    got = run(nc, [arrays], core_ids=[0]).results[0]["out"]
    return np.ascontiguousarray(np.asarray(got).reshape(B, T, D).transpose(0, 2, 1))
```

```python
from contextlib import ExitStack

import concourse.bass as bass
from concourse import mybir

F32, F32R, I32 = mybir.dt.float32, mybir.dt.float32r, mybir.dt.int32
ALU, ACT, AX = mybir.AluOpType, mybir.ActivationFunctionType, mybir.AxisListType

B, D, T, HEADS, TAPS = 8, 512, 1024, 8, 8
P = 128
DK = D // HEADS
DC = D // P
PAIRS = HEADS // 2
TT = T // P
SCALE = DK ** -0.5
NEG = -1e30
PACKED = 640
PAD = TAPS - 1
BANK = 512
S0, S1, X, O, XB = 0, 1, 2, 3, 4


class Memory:
    pass


class Plan:

    def __init__(self, cap):
        self.cap, self.nt, self.half = cap, cap // P, cap // 2
        short = cap < T
        self.n_ab = 4 if short else 2
        self.n_cd = 2 if short else 1
        self.n_hl = 2
        self.n_p = 2 if short else 1
        self.n_ps = 2 if short else 1
        self.n_raw = 2 if short else 1
        self.n_x1 = 2 if short else 1
        self.n_out = 2 if short else 1
        self.out_pairs = (self.nt + 1) // 2
        self.use, self.maxima_before, self.count = {}, {}, [0, 0, 0, 0, 0]
        nt = self.nt
        for c in range(DC):
            self._add(("T", c), (S0, S1, X, S0)[c])
        self._add(("Q", 0), S1)
        self._add(("Q", 1), X)
        for i in range(nt):
            self._add(("V", i), i % 2)
            self._add_maxima(0, self.first_max_tiles(i))
            if i == nt - 2:
                self._add(("MT", 0), X)
        for p in range(PAIRS):
            for i in range(nt):
                for hh in range(2):
                    self._add(("S", p, i, hh), hh)
                if p + 1 < PAIRS:
                    self._add_maxima(p + 1, self.max_tiles(i))
                if i == 0 and p < 2:
                    self._add(("Q", p + 2), X)
                if p and i == 1:
                    self._add(("DEN", p - 1), X)
                if p and i == 2:
                    self._add(("RB", p - 1), X)
                if p + 1 < PAIRS and i == nt - 3:
                    self._add(("MT", p + 1), X)
            self._add(("O", p), O)
        self._add(("DEN", PAIRS - 1), X)
        self._add(("RB", PAIRS - 1), X)
        for g in range(self.out_pairs):
            self._add(("W", g), g % 2)
        self._add(("MEAN",), X)
        self.adds = nt - 1 if self.n_p > 1 else nt

    def _add(self, key, slot):
        self.use[key] = (slot, self.count[slot])
        self.maxima_before[key] = self.count[XB]
        self.count[slot] += 1

    def _add_maxima(self, p, tiles):
        for t in tiles:
            self._add(("M", p, t, 0), X)
            self._add(("M", p, t, 1), XB)

    def max_tiles(self, i):
        n, steps = 2 * self.nt, self.nt - 2
        return range(n * i // steps, n * (i + 1) // steps) if i < steps else range(0)

    def first_max_tiles(self, i):
        n, steps = 2 * self.nt, self.nt - 2
        return range(n * (i - 1) // steps, n * i // steps) if 0 < i <= steps else range(0)

    def slot(self, key):
        return self.use[key][0]

    def before(self, b, key):
        return b * self.count[self.use[key][0]] + self.use[key][1]

    def after(self, b, key):
        return self.before(b, key) + 1

    def rounds(self, p, i):
        rest = (TAPS + 1) * (TT // 2)
        first = [6, 12, 18, 18 + 13]
        if p < PAIRS - 1:
            if i < self.nt - 2:
                return range(0)
            end = first[p]
            return range(end - 6, end - 3) if i == self.nt - 2 else range(end - 3, end)
        if i == self.nt:
            return range(first[3], rest)
        return range(18 + 13 * i // self.nt, 18 + 13 * (i + 1) // self.nt)

    def read(self, b, step):
        if step < 0:
            if isinstance(b, int) and b == 0:
                return 0
            return self.read(b, step + PAIRS * self.nt) - PAIRS * self.adds
        p, i = divmod(step, self.nt)
        return b * PAIRS * self.adds + p * self.adds + (max(i, 1) if self.n_p > 1 else i + 1)

    def ab_value(self, b, p):
        return 16 * 8 * (b * (PAIRS // self.n_ab) + p // self.n_ab + 1)

    def cd_value(self, b, p):
        return 16 * 6 * (b * (PAIRS // self.n_cd) + p // self.n_cd + 1)

    def max_value(self, b, p):
        return 16 * 2 * (b * (PAIRS // self.n_cd) + p // self.n_cd + 1)

    def out_value(self, b, g):
        per_batch = (self.out_pairs + self.n_out - g % self.n_out) // self.n_out
        return 16 * (b * per_batch + g // self.n_out + 1)

    def x1_value(self, c, k):
        return 16 * (c * (TT // 2 // self.n_x1) + k // self.n_x1 + 1)

    y_value = x1_value

    def last_out(self):
        return range(self.out_pairs + 1 - self.n_out, self.out_pairs + 1)


def wait(eng, sem, value):
    if not isinstance(value, int) or value > 0:
        eng.wait_ge(sem, value)


def batches(eng, body):
    body(0)
    body(1)
    with eng.Fori(2, B - 1) as b:
        body(b)
    body(B - 1)


def has_before(b):
    return not isinstance(b, int) or b > 0


def has_after(b):
    return not isinstance(b, int) or b < B - 1


def f32(ap):
    return ap.bitcast(F32)


def setup(nc, m):
    with ExitStack() as ctx:
        def sb(name, shape, dt=F32):
            return ctx.enter_context(nc.sbuf_tensor(name, shape, dt))

        def sem(name):
            return ctx.enter_context(nc.semaphore(name))

        wq_t, wo_t, wq_e = (sb(n, [P, DC, D]) for n in ("wq_t", "wo_t", "wq_e"))
        before = sb("before", [P, P])
        ones = sb("ones", [P, P])
        token_f, batch_at = sb("token_f", [P, B, TT]), sb("batch_at", [P, B, TT])
        batch_i = sb("batch_i", [P, B, TT], I32)
        order_i, order_f = sb("order_i", [B, T], I32), sb("order_f", [B, T])
        tail = sb("tail", [B, T])
        tile_sums, tile_base = sb("tile_sums", [P, B]), sb("tile_base", [P, B, TT])
        rank, place, spare = (sb(n, [P, B, TT]) for n in ("rank", "place", "spare"))
        n_valid, n_valid_row = sb("n_valid", [P, B]), sb("n_valid_row", [B, 1])
        most = sb("most", [P, 1])
        row_i = sb("row_i", [P, B, TT], I32)

        mask_in, weights_in, stored = sem("mask_in"), sem("weights_in"), sem("stored")
        iotas, blank, shapes_ready = sem("iotas"), sem("blank"), sem("shapes_ready")
        sums_ready, counted, chain, indices = sem("sums_ready"), sem("counted"), sem("chain"), sem("indices")
        high, mean_full, mean_out = sem("weights_high"), sem("mean_full"), sem("mean_out")
        mask3 = m.mask[:].rearrange("p (b j) -> p b j", b=B)
        prefix, totals = m.psum[S0][:, 0, 0:B * TT], m.psum[S0][:, 1, 0:B * TT]
        valid_all, valid_col = m.psum[X][:, 0, 0:B], m.psum[X][0:B, 1, 0:2]
        block = ctx.enter_context(nc.Block())

        @block.sync
        def _(sp):
            sp.dma_start(m.mask[:], m.maskT).then_inc(mask_in, 16)
            for dst, w in ((wq_t, m.wqT), (wo_t, m.woT), (wq_e, m.wq)):
                sp.dma_start(dst[:], w.rearrange("(c p) n -> p c n", p=P)).then_inc(weights_in, 16)
            sp.wait_ge(indices, 3)
            sp.dma_start(m.row_of.rearrange("b p j -> p b j"), row_i[:]).then_inc(stored, 16)
            sp.dma_start(m.tail_rows, tail[:]).then_inc(stored, 16)
            sp.wait_ge(stored, 32)

        @block.gpsimd
        def _(pool):
            nc.gpsimd.iota(m.token[:], [[T, B], [P, TT]], base=0, channel_multiplier=1).then_inc(iotas, 1)
            nc.gpsimd.iota(batch_i[:], [[T, B], [0, TT]], base=0, channel_multiplier=0).then_inc(iotas, 1)
            nc.gpsimd.iota(order_i[:], [[1, T]], base=0, channel_multiplier=0).then_inc(iotas, 1)
            nc.gpsimd.memset(ones[:], 1.0).then_inc(blank, 1)
            nc.gpsimd.memset(m.ident[:], 0.0).then_inc(blank, 1)
            nc.gpsimd.memset(m.one_column[:], 0.0).then_inc(blank, 1)
            pool.wait_ge(blank, 3)
            nc.gpsimd.affine_select(out=m.one_column[:], in_=m.one_column[:], compare_op=ALU.not_equal, fill=1.0,
                                    base=1 - 2 * TT, pattern=[[1, 4 * TT - 1]],
                                    channel_multiplier=0).then_inc(shapes_ready, 1)
            nc.gpsimd.affine_select(out=m.ident[:], in_=m.ident[:], compare_op=ALU.not_equal, fill=1.0, base=0,
                                    pattern=[[-1, P]], channel_multiplier=1).then_inc(shapes_ready, 1)
            nc.gpsimd.affine_select(out=before[:], in_=ones[:], compare_op=ALU.is_ge, fill=0.0, base=-1,
                                    pattern=[[1, P]], channel_multiplier=-1).then_inc(shapes_ready, 1)
            pool.wait_ge(indices, 1)
            for j in range(TT):
                scatter_tokens(nc, m, m.place_i[:, 0, :], m.token[:, 0, :], j)
            pool.wait_ge(m.scattered, 16 * TT)

        @block.tensor
        def _(pe):
            pe.wait_ge(mask_in, 16)
            pe.wait_ge(shapes_ready, 3)
            pe.wait_ge(sums_ready, 1)
            nc.tensor.matmul(prefix, before[:], m.mask[:], start=True, stop=True)
            nc.tensor.matmul(totals, ones[:], m.mask[:], start=True, stop=True)
            nc.tensor.matmul(valid_all, ones[:], tile_sums[:], start=True, stop=True)
            nc.tensor.matmul(valid_col, tile_sums[:], ones[:, 0:2], start=True, stop=True).then_inc(counted, 1)
            pe.wait_ge(weights_in, 48)
            for g in range(DC):
                for c in range(DC):
                    last = nc.tensor.matmul(m.psum[(S1, O)[g // 2]][:, g % 2, :], wq_e[:, c, g * P:(g + 1) * P],
                                            wo_t[:, c, :], start=c == 0, stop=c == DC - 1)
                last.then_inc(mean_full, 1)

        @block.scalar
        def _(act):
            act.wait_ge(weights_in, 48)
            nc.scalar.activation(m.wq_hi[:], wq_t[:], ACT.Copy).then_inc(high, 1)
            nc.scalar.activation(m.wo_hi[:], wo_t[:], ACT.Copy).then_inc(high, 1)
            for g in range(DC):
                act.wait_ge(mean_full, g + 1)
                nc.scalar.activation(m.w_mean[:, g, :], m.psum[(S1, O)[g // 2]][:, g % 2, :],
                                     ACT.Copy).then_inc(mean_out, 1)
            act.wait_ge(mean_out, DC)

        @block.vector
        def _(dve):
            done = [0]

            def link(ins):
                done[0] += 1
                ins.then_inc(chain, 1)
                dve.wait_ge(chain, done[0])

            dve.wait_ge(mask_in, 16)
            nc.vector.tensor_reduce(tile_sums[:], mask3, AX.X, ALU.add).then_inc(sums_ready, 1)
            nc.vector.tensor_scalar(m.last_tap[:], m.mask[:, (TAPS - 1) * TT:TAPS * TT], 1.0, None, ALU.add)
            dve.wait_ge(iotas, 3)
            nc.vector.tensor_copy(token_f[:], m.token[:])
            nc.vector.tensor_copy(batch_at[:], batch_i[:])
            nc.vector.tensor_copy(order_f[:], order_i[:])
            link(nc.vector.memset(tile_base[:], 0.0))
            dve.wait_ge(counted, 1)
            tot3 = totals.rearrange("p (b j) -> p b j", b=B)
            for j in range(1, TT):
                link(nc.vector.tensor_tensor(tile_base[:, :, j], tile_base[:, :, j - 1], tot3[:, :, j - 1], ALU.add))
            nc.vector.tensor_copy(n_valid[:], valid_all)
            nc.vector.tensor_copy(n_valid_row[:], valid_col[:, 0:1])
            link(nc.vector.tensor_tensor(rank[:], tile_base[:], prefix.rearrange("p (b j) -> p b j", b=B), ALU.add))
            link(nc.vector.tensor_tensor(spare[:], token_f[:], rank[:], ALU.subtract))
            for b in range(B):
                last = nc.vector.tensor_scalar(spare[:, b, :], spare[:, b, :], n_valid[:, b:b + 1], None, ALU.add)
            link(last)
            link(nc.vector.tensor_tensor(place[:], rank[:], batch_at[:], ALU.add))
            link(nc.vector.tensor_tensor(place[:], place[:], spare[:], ALU.subtract))
            link(nc.vector.tensor_tensor(place[:], place[:], mask3, ALU.mult))
            link(nc.vector.tensor_tensor(place[:], place[:], spare[:], ALU.add))
            nc.vector.tensor_copy(m.place_i[:], place[:]).then_inc(indices, 1)
            link(nc.vector.tensor_scalar(rank[:], rank[:], 1.0, None, ALU.add))
            link(nc.vector.tensor_tensor(rank[:], rank[:], mask3, ALU.mult))
            nc.vector.tensor_copy(row_i[:], rank[:]).then_inc(indices, 1)
            nc.vector.tensor_scalar(tail[:], order_f[:], n_valid_row[:], NEG, ALU.is_ge, ALU.mult).then_inc(indices, 1)
            for b in range(B):
                nc.vector.tensor_scalar(m.valid[:, b, :], token_f[:, 0, :], n_valid[:, b:b + 1], None, ALU.is_lt)
            link(nc.vector.tensor_reduce(most[:], n_valid[:], AX.X, ALU.max))
            nc.vector.tensor_copy(m.most_valid[:], most[:])
            dve.wait_ge(high, 2)
            nc.vector.tensor_tensor(m.wq_lo[:], wq_t[:], f32(m.wq_hi[:]), ALU.subtract)
            link(nc.vector.tensor_tensor(m.wo_lo[:], wo_t[:], f32(m.wo_hi[:]), ALU.subtract))


def scatter_tokens(nc, m, place, token, j):
    nc.gpsimd.indirect_dma_start(m.token_at, bass.IndirectOffsetOnAxis(ap=place[:, j:j + 1], axis=0),
                                 token[:, j:j + 1], None).then_inc(m.scattered, 16)


def path_memory(nc, m, plan):
    n = Memory()
    cap, nt = plan.cap, plan.nt
    with ExitStack() as ctx:
        def sb(name, shape, dt=F32):
            return ctx.enter_context(nc.sbuf_tensor(f"{name}_{cap}", shape, dt))

        n.packed_out = nc.dram_tensor(f"packed_out_{cap}", [1 + cap, D], F32, kind="Internal").ap()
        n.token_idx = sb("token_idx", [P, nt], I32)
        n.row_idx = sb("row_idx", [P, TT], I32)
        n.xg = sb("xg", [P, nt, D])
        n.xt_hi, n.xt_lo = sb("xt_hi", [P, DC, cap], F32R), sb("xt_lo", [P, DC, cap], F32R)
        n.q_hi, n.q_lo = sb("q_hi", [P, plan.n_hl, cap], F32R), sb("q_lo", [P, plan.n_hl, cap], F32R)
        n.ab = sb("ab", [P, plan.n_ab, 2, 2, cap], F32R)
        n.cd = sb("cd", [P, plan.n_cd, 2, 2, cap], F32R)
        n.prob = sb("prob", [P, plan.n_p, 2, cap])
        n.prob_sum = sb("prob_sum", [P, plan.n_ps, 2, cap])
        n.v = sb("v", [P, nt, D])
        n.neg_max = sb("neg_max", [P, 2, 2, 2 * nt])
        n.neg_row = sb("neg_row", [P, 2, 2 * nt])
        n.max_row = sb("max_row", [2 * nt, 2, P], F32R)
        n.raw = sb("raw", [P, plan.n_raw, cap])
        n.recip = sb("recip", [P, P])
        n.out_st = sb("out_st", [P, plan.n_out, 2, D])
        n.xbar = sb("xbar", [P, DC])
        n.x1 = sb("x1", [P, plan.n_x1, 2, PAD + D])
        n.g = sb("g", [P, 2, D])
        n.y = sb("y", [P, plan.n_x1, 2, D])
        n.xm = n.out_st[:, 0].rearrange("p a c -> p (a c)")
        n.place_now, n.token_now = sb("place_now", [P, TT], I32), sb("token_now", [P, TT], I32)
        n.valid_now = sb("valid_now", [P, TT])
    return n


def halves(ap, plan):
    return ap.rearrange("p (a c) -> p a c", a=2)


CONV_PAIR = 2 * (TAPS + 1)
CONV_BATCH = CONV_PAIR * (TT // 2)


def tensor_program(nc, pe, m, r, plan):
    nt, cap, half = plan.nt, plan.cap, plan.half

    def claim(b, key):
        wait(pe, m.free[plan.slot(key)], plan.before(b, key))
        if plan.slot(key) == X and key[0] != "M":
            wait(pe, m.free[XB], b * plan.count[XB] + plan.maxima_before[key])
        return m.psum[X if plan.slot(key) == XB else plan.slot(key)]

    def filled(ins, key):
        ins.then_inc(m.full[plan.slot(key)], 1)

    def project(b, p):
        q = claim(b, ("Q", p))
        for a in range(2):
            n = 0
            for c in range(DC):
                if p == 0 and a == 0:
                    pe.wait_ge(m.free[plan.slot(("T", c))], plan.after(b, ("T", c)))
                for w, xt in ((m.wq_hi, r.xt_hi), (m.wq_lo, r.xt_hi), (m.wq_hi, r.xt_lo)):
                    last = nc.tensor.matmul(q[:, a, 0:half], w[:, c, p * P:(p + 1) * P],
                                            xt[:, c, a * half:(a + 1) * half], start=n == 0, stop=n == 3 * DC - 1)
                    n += 1
        filled(last, ("Q", p))

    def maxima(b, p, tiles):
        ab = r.ab[:, p % plan.n_ab]
        for t in tiles:
            hh, i = divmod(t, nt)
            for a in range(2):
                s = claim(b, ("M", p, t, a))
                filled(nc.tensor.matmul(s[:, a, 0:half], ab[:, hh, 0, i * P:(i + 1) * P],
                                        ab[:, hh, 1, a * half:(a + 1) * half], start=True, stop=True),
                       ("M", p, t, a))

    def max_transpose(b, p):
        key = ("MT", p)
        s = claim(b, key)
        pe.wait_ge(m.maxima_taken, b * PAIRS + p + 1)
        filled(nc.tensor.transpose(s[0:2 * nt, 0, 0:P], r.neg_row[:, p % 2, :], m.ident[:]), key)

    def denominators(b, p):
        s = claim(b, ("DEN", p))
        for hh in range(2):
            pe.wait_ge(m.added[hh], (b * PAIRS + p + 1) * plan.adds)
        for t in range(2 * nt):
            hh, i = divmod(t, nt)
            last = nc.tensor.matmul(s[0:2 * nt, 0, 0:P], m.one_column[:, 2 * TT - 1 - t:2 * TT - 1 - t + 2 * nt],
                                    r.prob_sum[:, p % plan.n_ps, hh, i * P:(i + 1) * P],
                                    start=t == 0, stop=t == 2 * nt - 1)
        filled(last, ("DEN", p))

    def spread(b, p):
        s = claim(b, ("RB", p)).rearrange("p a c -> p (a c)")
        pe.wait_ge(m.recips, b * PAIRS + p + 1)
        for i in range(nt):
            for hh in range(2):
                row = m.ident[:, hh * nt + i:hh * nt + i + 1].to_broadcast([P, DK])
                last = nc.tensor.matmul(s[hh * DK:(hh + 1) * DK, i * P:(i + 1) * P], row, r.recip[:],
                                        start=True, stop=True)
        filled(last, ("RB", p))

    def context(b, p, i):
        if i == 0:
            claim(b, ("O", p))
        for hh in range(2):
            pe.wait_ge(m.free[hh], plan.after(b, ("S", p, i, hh)))
        step = p * nt + i
        for a in range(2):
            for hh in range(2):
                last = nc.tensor.matmul(m.psum[O][hh * DK:(hh + 1) * DK, a, 0:half],
                                        r.v[:, i, (2 * p + hh) * DK:(2 * p + hh + 1) * DK],
                                        r.prob[:, step % plan.n_p, hh, a * half:(a + 1) * half],
                                        start=i == 0, stop=i == nt - 1)
        last.then_inc(m.full[O], 1)

    def output_rows(b, g, pairs):
        w = claim(b, ("W", g)) if pairs[0] == 0 else m.psum[g % 2]
        for a in range(min(2, nt - 2 * g)):
            i = 2 * g + a
            for c in pairs:
                for n, (ct, wo) in enumerate(((r.xt_hi, m.wo_hi), (r.xt_lo, m.wo_hi), (r.xt_hi, m.wo_lo))):
                    last = nc.tensor.matmul(w[:, a, :], ct[:, c, i * P:(i + 1) * P], wo[:, c, :],
                                            start=c == 0 and n == 0, stop=c == PAIRS - 1 and n == 2)
        if pairs[-1] == PAIRS - 1:
            filled(last, ("W", g))

    def body(b):
        pe.wait_ge(m.rows_masked, (b + 1) * nt)
        for c in range(DC):
            s = claim(b, ("T", c)).rearrange("p a c -> p (a c)")
            for i in range(nt):
                last = nc.tensor.transpose(s[:, i * P:(i + 1) * P], r.xg[:, i, c * P:(c + 1) * P], m.ident[:])
            filled(last, ("T", c))
        project(b, 0)
        project(b, 1)
        for i in range(nt):
            v = claim(b, ("V", i))
            n = 0
            for xt, w in ((r.xt_hi, m.wq_hi), (r.xt_lo, m.wq_hi), (r.xt_hi, m.wq_lo)):
                for c in range(DC):
                    last = nc.tensor.matmul(v[:, 0, :], xt[:, c, i * P:(i + 1) * P], w[:, c, :],
                                            start=n == 0, stop=n == 3 * DC - 1)
                    n += 1
            filled(last, ("V", i))
            if i == 1:
                pe.wait_ge(m.ab_in[0], plan.ab_value(b, 0))
            maxima(b, 0, plan.first_max_tiles(i))
            if i == nt - 2:
                max_transpose(b, 0)
        previous = None
        for p in range(PAIRS):
            ab, cd = r.ab[:, p % plan.n_ab], r.cd[:, p % plan.n_cd]
            for i in range(nt):
                if i == 0:
                    pe.wait_ge(m.ab_in[p % plan.n_ab], plan.ab_value(b, p))
                    pe.wait_ge(m.cd_in[p % plan.n_cd], plan.cd_value(b, p))
                    pe.wait_ge(m.max_in[p % plan.n_cd], plan.max_value(b, p))
                tiles = plan.max_tiles(i) if p + 1 < PAIRS else range(0)
                for hh in range(2):
                    s = claim(b, ("S", p, i, hh))
                    for a in range(2):
                        cols = slice(a * half, (a + 1) * half)
                        nc.tensor.matmul(s[:, a, 0:half], ab[:, hh, 0, i * P:(i + 1) * P], ab[:, hh, 1, cols],
                                         start=True, stop=False)
                        last = nc.tensor.matmul(s[:, a, 0:half], cd[:, hh, 0, i * P:(i + 1) * P],
                                                cd[:, hh, 1, cols], start=False, stop=True)
                    filled(last, ("S", p, i, hh))
                    if p + 1 < PAIRS and i == 0 and hh == 0:
                        pe.wait_ge(m.ab_in[(p + 1) % plan.n_ab], plan.ab_value(b, p + 1))
                    maxima(b, p + 1, tiles[hh:hh + 1])
                if previous:
                    context(b, *previous)
                previous = (p, i)
                maxima(b, p + 1, tiles[2:])
                if i == 0 and p < 2:
                    project(b, p + 2)
                if p and i == 1:
                    denominators(b, p - 1)
                if p and i == 2:
                    spread(b, p - 1)
                if p + 1 < PAIRS and i == nt - 3:
                    max_transpose(b, p + 1)
        context(b, *previous)
        opened = min(2, plan.out_pairs)
        pe.wait_ge(m.ctx_split, b * PAIRS + PAIRS - 1)
        for g in range(opened):
            output_rows(b, g, range(PAIRS - 1))
            if g == 0:
                denominators(b, PAIRS - 1)
        spread(b, PAIRS - 1)
        pe.wait_ge(m.channel_mean, (b + 1) * DC)
        pe.wait_ge(m.ctx_split, (b + 1) * PAIRS)
        for g in range(plan.out_pairs):
            output_rows(b, g, range(PAIRS - 1, PAIRS) if g < opened else range(PAIRS))
        s = claim(b, ("MEAN",))
        for c in range(DC):
            last = nc.tensor.matmul(s[0:1, 0, :], r.xbar[:, c:c + 1], m.w_mean[:, c, :],
                                    start=c == 0, stop=c == DC - 1)
        filled(last, ("MEAN",))

    batches(pe, body)


def scalar_program(nc, act, m, r, plan):
    nt, cap, half = plan.nt, plan.cap, plan.half

    def ready(b, key):
        act.wait_ge(m.full[plan.slot(key)], plan.after(b, key))
        return m.psum[plan.slot(key)]

    def drained(ins, key):
        ins.then_inc(m.free[plan.slot(key)], 1)

    def mask_rows(b, i):
        if i == 0:
            act.wait_ge(m.rows_in, 16 * nt * (b + 1))
            act.wait_ge(m.valid_ready, 3 * b + 1)
        nc.scalar.activation(r.xg[:, i, :], r.xg[:, i, :], ACT.Copy,
                             scale=r.valid_now[:, i:i + 1]).then_inc(m.rows_masked, 1)

    def high_of_projection(b, p):
        s = ready(b, ("Q", p))
        if p >= plan.n_hl:
            act.wait_ge(m.ab_in[(p - plan.n_hl) % plan.n_ab], plan.ab_value(b, p - plan.n_hl))
            act.wait_ge(m.cd_in[(p - plan.n_hl) % plan.n_cd], plan.cd_value(b, p - plan.n_hl))
        elif has_before(b):
            old = p - plan.n_hl + PAIRS
            act.wait_ge(m.ab_in[old % plan.n_ab], plan.ab_value(b - 1, old))
            act.wait_ge(m.cd_in[old % plan.n_cd], plan.cd_value(b - 1, old))
        nc.scalar.activation(halves(r.q_hi[:, p % plan.n_hl, :], plan), s[:, :, 0:half],
                             ACT.Copy).then_inc(m.high, 1)

    def max_row(b, p):
        s = ready(b, ("MT", p))
        if p >= 2:
            act.wait_ge(m.max_in[(p - 2) % plan.n_cd], plan.max_value(b, p - 2))
        elif has_before(b):
            act.wait_ge(m.max_in[(p + 2) % plan.n_cd], plan.max_value(b - 1, p + 2))
        drained(nc.scalar.activation(r.max_row[:, p % 2, :], s[0:2 * nt, 0, 0:P], ACT.Copy), ("MT", p))

    def body(b):
        if not has_before(b):
            for i in range(nt):
                mask_rows(0, i)
        for c in range(DC):
            s = ready(b, ("T", c)).rearrange("p a c -> p (a c)")
            nc.scalar.activation(r.xt_hi[:, c, :], s[:, 0:cap], ACT.Copy).then_inc(m.high, 1)
        high_of_projection(b, 0)
        high_of_projection(b, 1)
        for i in range(nt):
            s = ready(b, ("V", i))
            drained(nc.scalar.activation(r.v[:, i, :], s[:, 0, :], ACT.Copy), ("V", i))
            if i == nt - 2:
                max_row(b, 0)
        for p in range(PAIRS):
            for i in range(nt):
                step = p * nt + i
                for hh in range(2):
                    s = ready(b, ("S", p, i, hh))
                    wait(act, m.full[O], b * PAIRS * nt + step - plan.n_p + 1)
                    wait(act, m.added[hh], plan.read(b, step - plan.n_p))
                    drained(nc.scalar.activation(halves(r.prob[:, step % plan.n_p, hh, :], plan),
                                                 s[:, :, 0:half], ACT.Exp, scale=SCALE), ("S", p, i, hh))
                if i == 0 and p:
                    raw_context(b, p - 1)
                if i == 0 and p < 2:
                    high_of_projection(b, p + 2)
                if i == 2 and p:
                    high_of_context(b, p - 1)
                if i == 1:
                    channel_mean(b, p)
                if p == PAIRS - 1 and has_after(b):
                    mask_rows(b + 1, i)
                if i == nt - 3 and p + 1 < PAIRS:
                    max_row(b, p + 1)
        raw_context(b, PAIRS - 1)
        high_of_context(b, PAIRS - 1)
        for g in range(plan.out_pairs):
            s = ready(b, ("W", g))
            tiles = min(2, nt - 2 * g)
            wait(act, m.out_stored[g % plan.n_out], plan.out_value(b, g) - 16)
            drained(nc.scalar.activation(r.out_st[:, g % plan.n_out, 0:tiles, :], s[:, 0:tiles, :], ACT.Copy),
                    ("W", g))
        s = ready(b, ("MEAN",))
        g = plan.out_pairs
        wait(act, m.out_stored[g % plan.n_out], plan.out_value(b, g) - 16)
        drained(nc.scalar.activation(r.out_st[0:1, g % plan.n_out, 0, :], s[0:1, 0, :], ACT.Copy), ("MEAN",))

    def raw_context(b, p):
        act.wait_ge(m.full[O], (b * PAIRS + p + 1) * nt)
        wait(act, m.ctx_split, b * PAIRS + p - plan.n_raw + 1)
        nc.scalar.activation(halves(r.raw[:, p % plan.n_raw, :], plan), m.psum[O][:, :, 0:half],
                             ACT.Copy).then_inc(m.free[O], 1)

    def high_of_context(b, p):
        act.wait_ge(m.free[X], plan.after(b, ("RB", p)))
        nc.scalar.activation(r.xt_hi[:, p, :], r.raw[:, p % plan.n_raw, :], ACT.Copy).then_inc(m.high, 1)

    def channel_mean(b, c):
        act.wait_ge(m.xm_in, 16 * (b * DC + c + 1))
        nc.scalar.activation(r.xm, r.xm, ACT.Copy, scale=1.0 / T,
                             accum_out=r.xbar[:, c:c + 1]).then_inc(m.channel_mean, 1)

    batches(act, body)


def vector_program(nc, dve, m, r, plan):
    nt, cap, half = plan.nt, plan.cap, plan.half

    def ready(b, key):
        dve.wait_ge(m.full[plan.slot(key)], plan.after(b, key))
        return m.psum[plan.slot(key)]

    def drained(ins, key):
        ins.then_inc(m.free[plan.slot(key)], 1)

    def low_of_projection(b, p):
        s = ready(b, ("Q", p))
        dve.wait_ge(m.high, b * (DC + 2 * PAIRS) + DC + p + 1)
        drained(nc.vector.tensor_tensor(halves(r.q_lo[:, p % plan.n_hl, :], plan), s[:, :, 0:half],
                                        halves(f32(r.q_hi[:, p % plan.n_hl, :]), plan), ALU.subtract), ("Q", p))

    def maxima(b, p, tiles):
        for t in tiles:
            for a in range(2):
                dve.wait_ge(m.full[(X, XB)[a]], plan.after(b, ("M", p, t, a)))
                drained(nc.vector.tensor_reduce(r.neg_max[:, p % 2, a, t:t + 1], m.psum[X][:, a, 0:half], AX.X,
                                                ALU.max, negate=True), ("M", p, t, a))
        if len(tiles) and tiles[-1] == 2 * nt - 1:
            dve.wait_ge(m.free[XB], plan.after(b, ("M", p, 2 * nt - 1, 1)))
            nc.vector.tensor_tensor(r.neg_row[:, p % 2, :], r.neg_max[:, p % 2, 0, :], r.neg_max[:, p % 2, 1, :],
                                    ALU.min).then_inc(m.maxima_taken, 1)

    def reciprocals(b, p):
        s = ready(b, ("DEN", p))
        drained(nc.vector.tensor_scalar(r.recip[0:2 * nt, :], s[0:2 * nt, 0, 0:P], 1e-30, None, ALU.max), ("DEN", p))
        dve.wait_ge(m.free[X], plan.after(b, ("DEN", p)))
        nc.vector.reciprocal(r.recip[0:2 * nt, :], r.recip[0:2 * nt, :]).then_inc(m.recips, 1)

    def normalise(b, p):
        s = ready(b, ("RB", p)).rearrange("p a c -> p (a c)")
        dve.wait_ge(m.free[O], b * PAIRS + p + 1)
        raw = r.raw[:, p % plan.n_raw, :]
        drained(nc.vector.tensor_tensor(raw, raw, s[:, 0:cap], ALU.mult), ("RB", p))

    def low_of_context(b, p):
        dve.wait_ge(m.high, b * (DC + 2 * PAIRS) + DC + PAIRS + p + 1)
        nc.vector.tensor_tensor(r.xt_lo[:, p, :], r.raw[:, p % plan.n_raw, :], f32(r.xt_hi[:, p, :]),
                                ALU.subtract).then_inc(m.ctx_split, 1)

    def conv_round(c, n):
        k, step = divmod(n, TAPS + 1)
        x1, y = r.x1[:, k % plan.n_x1], r.y[:, k % plan.n_x1]
        done = c * CONV_BATCH + k * CONV_PAIR
        if step == 0:
            dve.wait_ge(m.x1_in[k % plan.n_x1], plan.x1_value(c, k))
            dve.wait_ge(m.g_in, 32 * (c * (TT // 2) + k + 1))
        if step == 1:
            wait(dve, m.y_stored[k % plan.n_x1], plan.y_value(c, k) - 16)
        for u in range(2):
            if step:
                dve.wait_ge(m.conv, done + 2 * step - 1 + u)
            if step == 0:
                ins = nc.vector.tensor_tensor(x1[:, u, PAD:PAD + D], x1[:, u, PAD:PAD + D], r.g[:, u, :], ALU.add)
            elif step == 1:
                ins = nc.vector.tensor_scalar(y[:, u, :], x1[:, u, PAD:PAD + D],
                                              m.last_tap[:, 2 * k + u:2 * k + u + 1], None, ALU.mult)
            else:
                tap = step - 2
                j = tap * TT + 2 * k + u
                ins = nc.vector.scalar_tensor_tensor(y[:, u, :], x1[:, u, tap:tap + D], m.mask[:, j:j + 1],
                                                     y[:, u, :], ALU.mult, ALU.add)
            ins.then_inc(m.conv, 1)

    def body(b):
        if isinstance(b, int) and b == 0:
            nc.vector.memset(r.x1[:], 0.0).then_inc(m.zeroed, 1)
            nc.vector.memset(r.recip[:], 0.0).then_inc(m.zeroed, 1)
            for n in range(plan.n_cd):
                for hh in range(2):
                    nc.vector.memset(f32(r.cd[DK:P, n, hh, 0, :]), 0.0).then_inc(m.zeroed, 1)
                    nc.vector.memset(f32(r.cd[DK:P, n, hh, 1, :]), 1.0).then_inc(m.zeroed, 1)
            dve.wait_ge(m.zeroed, 2 + 4 * plan.n_cd)
            for n in range(plan.n_cd):
                for hh in range(2):
                    nc.vector.memset(f32(r.cd[DK:DK + 1, n, hh, 0, :]), 1.0).then_inc(m.zeroed, 1)
            nc.vector.tensor_copy(r.valid_now[:], m.valid[:, 0, :]).then_inc(m.valid_ready, 1)
        for c in range(DC):
            s = ready(b, ("T", c)).rearrange("p a c -> p (a c)")
            dve.wait_ge(m.high, b * (DC + 2 * PAIRS) + c + 1)
            drained(nc.vector.tensor_tensor(r.xt_lo[:, c, :], s[:, 0:cap], f32(r.xt_hi[:, c, :]), ALU.subtract),
                    ("T", c))
        if has_after(b):
            nxt = slice(b + 1, b + 2) if isinstance(b, int) else bass.ds(b + 1, 1)
            for now, every in ((r.place_now, m.place_i), (r.token_now, m.token), (r.valid_now, m.valid)):
                last = nc.vector.tensor_copy(now[:], every[:, nxt, :].rearrange("p o j -> p (o j)"))
                last.then_inc(m.valid_ready, 1)
        low_of_projection(b, 0)
        low_of_projection(b, 1)
        for i in range(nt):
            maxima(b, 0, plan.first_max_tiles(i))
        for p in range(PAIRS):
            for i in range(nt):
                if p + 1 < PAIRS:
                    maxima(b, p + 1, plan.max_tiles(i))
                if i == 0 and p < 2:
                    low_of_projection(b, p + 2)
                if p and i == 1:
                    reciprocals(b, p - 1)
                if p and i == 2:
                    normalise(b, p - 1)
                if p and i == 2:
                    low_of_context(b, p - 1)
                if has_before(b):
                    for n in plan.rounds(p, i):
                        conv_round(b - 1, n)
        reciprocals(b, PAIRS - 1)
        normalise(b, PAIRS - 1)
        low_of_context(b, PAIRS - 1)
        if has_before(b):
            for n in plan.rounds(PAIRS - 1, nt):
                conv_round(b - 1, n)

    batches(dve, body)
    for n in range((TAPS + 1) * (TT // 2)):
        conv_round(B - 1, n)


def gpsimd_program(nc, pool, m, r, plan):
    nt = plan.nt

    def hold(sem, value):
        if not isinstance(value, int) or value > 0:
            pool.wait_ge(sem, value)
            pool.sem_inc(m.pool_passed, 1)

    def gather_rows(b):
        hold(m.tokens_in, 16 * (b + 1))
        if has_before(b):
            hold(m.full[plan.slot(("T", DC - 1))], plan.after(b - 1, ("T", DC - 1)))
        for i in range(nt):
            nc.gpsimd.indirect_dma_start(r.xg[:, i, :], None, m.xT,
                                         bass.IndirectOffsetOnAxis(ap=r.token_idx[:, i:i + 1], axis=0)
                                         ).then_inc(m.rows_in, 16)

    def gather_outputs(c, k):
        if k == 0:
            hold(m.out_rows_in, 16 * (c + 1))
            for g in plan.last_out():
                hold(m.out_stored[g % plan.n_out], plan.out_value(c, g))
        hold(m.conv, c * CONV_BATCH + (CONV_PAIR * (k - 1) + 2 if k else 0))
        for u in range(2):
            nc.gpsimd.indirect_dma_start(r.g[:, u, :], None, r.packed_out,
                                         bass.IndirectOffsetOnAxis(ap=r.row_idx[:, 2 * k + u:2 * k + u + 1], axis=0)
                                         ).then_inc(m.g_in, 16)

    def body(b):
        if isinstance(b, int) and b == 0:
            gather_rows(0)
        for p in range(PAIRS):
            for i in range(nt):
                step = p * nt + i
                if i == 0:
                    if p >= plan.n_ps:
                        pool.wait_ge(m.full[X], plan.after(b, ("DEN", p - plan.n_ps)))
                    elif has_before(b):
                        pool.wait_ge(m.full[X], plan.after(b - 1, ("DEN", p - plan.n_ps + PAIRS)))
                for hh in range(2):
                    total = r.prob_sum[:, p % plan.n_ps, hh, :]
                    now = r.prob[:, step % plan.n_p, hh, :]
                    if i or plan.n_p == 1:
                        hold(m.free[hh], plan.after(b, ("S", p, i, hh)))
                    if i == 0:
                        if plan.n_p == 1:
                            nc.gpsimd.tensor_copy(total, now).then_inc(m.added[hh], 1)
                        continue
                    wait(pool, m.added[hh], plan.read(b, step) - 1)
                    first = r.prob[:, (step - 1) % plan.n_p, hh, :] if i == 1 and plan.n_p > 1 else total
                    nc.gpsimd.tensor_tensor(total, first, now, ALU.add).then_inc(m.added[hh], 1)
                if i == 1 and has_before(b):
                    gather_outputs(b - 1, p)
            if p == 0 and has_after(b):
                hold(m.valid_ready, 3 * b + 4)
                for j in range(TT):
                    scatter_tokens(nc, m, r.place_now, r.token_now, j)
            if p == 2 and has_after(b):
                gather_rows(b + 1)

    batches(pool, body)
    for k in range(TT // 2):
        gather_outputs(B - 1, k)


def sync_program(nc, sp, m, r, plan):
    nt, cap = plan.nt, plan.cap

    def hold(sem, value):
        if not isinstance(value, int) or value > 0:
            sp.wait_ge(sem, value)
            sp.sem_inc(m.sync_passed, 1)

    def tokens(b):
        if has_before(b):
            hold(m.scattered, 16 * TT * (b + 1))
            hold(m.rows_in, 16 * nt * b)
        sp.dma_start(r.token_idx[:], m.token_at3[b].rearrange("(j p) -> p j", p=P)[:, 0:nt],
                     allow_slow_non_contiguous=True).then_inc(m.tokens_in, 16)

    def first_operands(b, p):
        buf = p % plan.n_ab
        hold(m.free[plan.slot(("Q", p))], plan.after(b, ("Q", p)))
        if p >= plan.n_ab:
            hold(m.full[S1], plan.after(b, ("S", p - plan.n_ab, nt - 1, 1)))
        elif has_before(b):
            hold(m.full[S1], plan.after(b - 1, ("S", p - plan.n_ab + PAIRS, nt - 1, 1)))
        for hh in range(2):
            rows = slice(hh * DK, (hh + 1) * DK)
            hi, lo = f32(r.q_hi[rows, p % plan.n_hl, :]), f32(r.q_lo[rows, p % plan.n_hl, :])
            for lower, which, part in ((0, 0, hi), (1, 0, lo), (0, 1, hi), (1, 1, hi)):
                sp.dma_start(f32(r.ab[lower * DK:(lower + 1) * DK, buf, hh, which, :]), part
                             ).then_inc(m.ab_in[buf], 16)

    def second_operands(b, p):
        buf = p % plan.n_cd
        hold(m.free[plan.slot(("Q", p))], plan.after(b, ("Q", p)))
        if p >= plan.n_cd:
            hold(m.full[S1], plan.after(b, ("S", p - plan.n_cd, nt - 1, 1)))
        elif has_before(b):
            hold(m.full[S1], plan.after(b - 1, ("S", p - plan.n_cd + PAIRS, nt - 1, 1)))
        else:
            hold(m.zeroed, 2 + 6 * plan.n_cd)
        for hh in range(2):
            rows = slice(hh * DK, (hh + 1) * DK)
            sp.dma_start(f32(r.cd[0:DK, buf, hh, 0, :]), f32(r.q_hi[rows, p % plan.n_hl, :])
                         ).then_inc(m.cd_in[buf], 16)
            sp.dma_start(f32(r.cd[0:DK, buf, hh, 1, :]), f32(r.q_lo[rows, p % plan.n_hl, :])
                         ).then_inc(m.cd_in[buf], 16)
            sp.dma_start(f32(r.cd[DK + 1:DK + 2, buf, hh, 0, :]), m.tail_rows[bass.ds(b, 1), 0:cap]
                         ).then_inc(m.cd_in[buf], 16)

    def max_rows(b, p):
        buf = p % plan.n_cd
        hold(m.free[X], plan.after(b, ("MT", p)))
        for hh in range(2):
            sp.dma_start(f32(r.cd[DK:DK + 1, buf, hh, 1, :]).rearrange("o (i q) -> o i q", i=nt),
                         f32(r.max_row[hh * nt:(hh + 1) * nt, p % 2, :])).then_inc(m.max_in[buf], 16)

    def conv_load(c, k):
        hold(m.conv, c * CONV_BATCH + (k + 1 - plan.n_x1) * CONV_PAIR if k + 1 >= plan.n_x1 else c * CONV_BATCH)
        if k == 0 and isinstance(c, int) and c == 0:
            hold(m.zeroed, 1)
        sp.dma_start(r.x1[:, k % plan.n_x1, :, PAD:PAD + D], m.xT4[c * (TT // 2) + k]
                     ).then_inc(m.x1_in[k % plan.n_x1], 16)

    def conv_store(c, k):
        hold(m.conv, c * CONV_BATCH + (k + 1) * CONV_PAIR)
        sp.dma_start(m.out4[c * (TT // 2) + k], r.y[:, k % plan.n_x1]).then_inc(m.y_stored[k % plan.n_x1], 16)

    def conv_traffic(b, p):
        c, following = b - 1, p + plan.n_x1 - 1
        if p:
            conv_store(c, p - 1)
        if 0 < following < TT // 2:
            conv_load(c, following)

    def mean_load(b, c):
        if c == 0 and has_before(b):
            for g in plan.last_out():
                hold(m.out_stored[g % plan.n_out], plan.out_value(b - 1, g))
        hold(m.channel_mean, b * DC + c)
        sp.dma_start(r.xm, m.x4[b * DC + c]).then_inc(m.xm_in, 16)

    def output_rows(c):
        hold(m.g_in, 32 * (TT // 2) * c)
        sp.dma_start(r.row_idx[:], m.row_of[c]).then_inc(m.out_rows_in, 16)

    def body(b):
        if isinstance(b, int) and b == 0:
            tokens(0)
        mean_load(b, 0)
        first_operands(b, 0)
        second_operands(b, 0)
        if has_before(b):
            output_rows(b - 1)
        first_operands(b, 1)
        if plan.n_cd > 1:
            second_operands(b, 1)
        max_rows(b, 0)
        for p in range(PAIRS):
            if p < 2:
                if p + 2 < plan.n_ab:
                    first_operands(b, p + 2)
            if p and p + 1 < PAIRS and plan.n_ab <= p + 1:
                first_operands(b, p + 1)
            if p and p + 1 < PAIRS and plan.n_cd > 1:
                second_operands(b, p + 1)
            if has_before(b) and p == 0:
                conv_load(b - 1, 0)
            if p + 1 < DC:
                mean_load(b, p + 1)
            if p == 1 and has_after(b):
                tokens(b + 1)
            if p + 1 < PAIRS:
                if plan.n_cd == 1:
                    second_operands(b, p + 1)
                max_rows(b, p + 1)
            if has_before(b):
                conv_traffic(b, p)
        hold(m.g_in, 32 * (TT // 2) * b)
        for g in range(plan.out_pairs):
            hold(m.free[g % 2], plan.after(b, ("W", g)))
            tiles = min(2, nt - 2 * g)
            rows = r.packed_out[1 + 2 * g * P:1 + (2 * g + tiles) * P, :]
            sp.dma_start(rows.rearrange("(a p) d -> p a d", p=P), r.out_st[:, g % plan.n_out, 0:tiles, :]
                         ).then_inc(m.out_stored[g % plan.n_out], 16)
        hold(m.free[X], plan.after(b, ("MEAN",)))
        g = plan.out_pairs
        sp.dma_start(r.packed_out[0:1, :], r.out_st[0:1, g % plan.n_out, 0, :]
                     ).then_inc(m.out_stored[g % plan.n_out], 16)
        if has_before(b):
            conv_store(b - 1, PAIRS - 1)

    batches(sp, body)
    output_rows(B - 1)
    conv_load(B - 1, 0)
    for k in range(TT // 2):
        if k + 1 < TT // 2 and plan.n_x1 > 1:
            conv_load(B - 1, k + 1)
        conv_store(B - 1, k)
        if k + 1 < TT // 2 and plan.n_x1 == 1:
            conv_load(B - 1, k + 1)
    for k in range(TT // 2 - plan.n_x1, TT // 2):
        hold(m.y_stored[k % plan.n_x1], plan.y_value(B - 1, k))


def cond_attn_conv(nc, xT, x, maskT, wqT, woT, wq, out):
    with ExitStack() as ctx:
        def sb(name, shape, dt=F32):
            return ctx.enter_context(nc.sbuf_tensor(name, shape, dt))

        def sem(name):
            return ctx.enter_context(nc.semaphore(name))

        def sems(name, n):
            return [sem(f"{name}{i}") for i in range(n)]

        m = Memory()
        m.xT, m.maskT, m.wqT, m.woT, m.wq = xT, maskT, wqT, woT, wq
        m.xT4 = xT.rearrange("(n u p) d -> n p u d", p=P, u=2)
        m.x4 = x.rearrange("(n p) t -> n p t", p=P)
        m.out4 = out.rearrange("(n u p) d -> n p u d", p=P, u=2)
        m.token_at = nc.dram_tensor("token_at", [B * T, 1], I32, kind="Internal").ap()
        m.token_at3 = m.token_at.rearrange("(b t) o -> b (t o)", b=B)
        m.row_of = nc.dram_tensor("row_of", [B, P, TT], I32, kind="Internal").ap()
        m.tail_rows = nc.dram_tensor("tail_rows", [B, T], F32, kind="Internal").ap()

        m.mask = sb("mask", [P, B * TT])
        m.wq_hi, m.wq_lo = sb("wq_hi", [P, DC, D], F32R), sb("wq_lo", [P, DC, D], F32R)
        m.wo_hi, m.wo_lo = sb("wo_hi", [P, DC, D], F32R), sb("wo_lo", [P, DC, D], F32R)
        m.w_mean = sb("w_mean", [P, DC, D])
        m.ident = sb("ident", [P, P])
        m.one_column = sb("one_column", [P, 4 * TT - 1])
        m.valid = sb("valid", [P, B, TT])
        m.last_tap = sb("last_tap", [P, TT])
        m.place_i, m.token = sb("place_i", [P, B, TT], I32), sb("token", [P, B, TT], I32)
        m.most_valid = sb("most_valid", [P, 1], I32)
        m.psum = [ctx.enter_context(nc.psum_tensor(f"slot{n}", [P, 2, BANK], F32)) for n in range(4)]
        m.scattered, m.zeroed, m.valid_ready = sem("scattered"), sem("zeroed"), sem("valid_ready")
        m.recips, m.ctx_split, m.conv, m.maxima_taken = (
            sem("recips"), sem("ctx_split"), sem("conv"), sem("maxima_taken"))
        m.rows_masked, m.high, m.channel_mean = sem("rows_masked"), sem("high"), sem("channel_mean")
        m.sync_passed, m.pool_passed = sem("sync_passed"), sem("pool_passed")
        m.tokens_in, m.rows_in, m.xm_in = sem("tokens_in"), sem("rows_in"), sem("xm_in")
        m.out_rows_in, m.g_in = sem("out_rows_in"), sem("g_in")
        m.x1_in, m.y_stored = sems("x1_in", 2), sems("y_stored", 2)
        m.full, m.free = sems("full", 5), sems("free", 5)
        m.added = sems("added", 2)
        m.ab_in, m.cd_in, m.max_in = sems("ab_in", 4), sems("cd_in", 2), sems("max_in", 2)
        m.out_stored = sems("out_stored", 2)

        setup(nc, m)
        short, full = ((path_memory(nc, m, plan), plan) for plan in (Plan(PACKED), Plan(T)))
        block = ctx.enter_context(nc.Block())

        @block.tensor
        def _(pe):
            fits = pe.value_load(m.most_valid[0:1, 0:1])
            with pe.If(fits < PACKED + 1):
                tensor_program(nc, pe, m, *short)
            with pe.Else():
                tensor_program(nc, pe, m, *full)

        @block.scalar
        def _(act):
            fits = act.value_load(m.most_valid[0:1, 0:1])
            with act.If(fits < PACKED + 1):
                scalar_program(nc, act, m, *short)
            with act.Else():
                scalar_program(nc, act, m, *full)

        @block.vector
        def _(dve):
            fits = dve.value_load(m.most_valid[0:1, 0:1])
            with dve.If(fits < PACKED + 1):
                vector_program(nc, dve, m, *short)
            with dve.Else():
                vector_program(nc, dve, m, *full)

        @block.gpsimd
        def _(pool):
            fits = pool.value_load(m.most_valid[0:1, 0:1])
            with pool.If(fits < PACKED + 1):
                gpsimd_program(nc, pool, m, *short)
            with pool.Else():
                gpsimd_program(nc, pool, m, *full)

        @block.sync
        def _(sp):
            fits = sp.value_load(m.most_valid[0:1, 0:1])
            with sp.If(fits < PACKED + 1):
                sync_program(nc, sp, m, *short)
            with sp.Else():
                sync_program(nc, sp, m, *full)


def kernel(x, cond_2048, L0_cond_Wq, L0_cond_Wo):
    import numpy as np
    import concourse.bacc as bacc
    from concourse.bass_utils import run_bass_kernel_spmd as run

    x, cond, wq, wo = (np.ascontiguousarray(a) for a in (x, cond_2048, L0_cond_Wq, L0_cond_Wo))
    arrays = {
        "xT": np.ascontiguousarray(x.transpose(0, 2, 1)).reshape(B * T, D),
        "x": x.reshape(B * D, T),
        "maskT": np.ascontiguousarray(cond.reshape(B * TT, P).T),
        "wqT": np.ascontiguousarray(wq.T),
        "woT": np.ascontiguousarray(wo.T),
        "wq": wq,
    }
    nc = bacc.Bacc("TRN2", target_bir_lowering=False, num_devices=1)
    args = [nc.dram_tensor(name, a.shape, F32, kind="ExternalInput").ap() for name, a in arrays.items()]
    out = nc.dram_tensor("out", [B * T, D], F32, kind="ExternalOutput").ap()
    cond_attn_conv(nc, *args, out)
    got = run(nc, [arrays], core_ids=[0]).results[0]["out"]
    return np.ascontiguousarray(np.asarray(got).reshape(B, T, D).transpose(0, 2, 1))
```

```python
from contextlib import ExitStack

import concourse.bass as bass
from concourse import mybir

F32, F32R, I32 = mybir.dt.float32, mybir.dt.float32r, mybir.dt.int32
ALU, ACT, AX = mybir.AluOpType, mybir.ActivationFunctionType, mybir.AxisListType

B, D, T, HEADS, TAPS = 8, 512, 1024, 8, 8
P = 128
DK = D // HEADS
DC = D // P
PAIRS = HEADS // 2
TT = T // P
SCALE = DK ** -0.5
NEG = -1e30
PACKED = 640
PAD = TAPS - 1
BANK = 512
ROUNDS = 3, 3, 10, 4
LATE = 5, 3, 1
S0, S1, X, O, XB = 0, 1, 2, 3, 4


class Memory:
    pass


class Plan:

    def __init__(self, cap):
        self.cap, self.nt, self.half = cap, cap // P, cap // 2
        short = cap < T
        self.early = PAIRS if short else 2
        self.den_step = 2 if short else 1
        self.n_ab = 4 if short else 2
        self.n_cd = 2 if short else 1
        self.n_hl = 2
        self.n_p = 2 if short else 1
        self.n_ps = 2 if short else 1
        self.n_raw = 2 if short else 1
        self.n_x1 = 2 if short else 1
        self.n_out = 2 if short else 1
        self.out_pairs = (self.nt + 1) // 2
        self.use, self.maxima_before, self.count = {}, {}, [0, 0, 0, 0, 0]
        nt = self.nt
        last = (self.out_pairs - 1) % 2
        self.last_slots = (1 - last, last)
        for c in range(DC):
            self._add(("T", c), ((X, O) + self.last_slots)[c])
        self._add(("Q", 0), X)
        self._add(("Q", 1), S0)
        self._add(("V", 0), S1)
        if self.early == PAIRS:
            self._add(("Q", 2), O)
            self._add_maxima(0, range(2 * nt))
            self._add(("V", 1), S1)
            self._add(("Q", 3), S0)
            self._add_maxima(0, range(2 * nt, 4 * nt))
            self._add(("V", 2), S1)
            self._add(("MT", 0), X)
            self._add(("V", 3), O)
        else:
            self._add_maxima(0, range(4 * nt))
            self._add(("V", 1), S1)
            self._add(("MT", 0), X)
        self.early_o = self.count[O]
        for p in range(PAIRS):
            for i in range(nt):
                for hh in range(2):
                    self._add(("S", p, i, hh), hh)
                if p and i == self.den_step:
                    self._add(("DEN", p - 1), X)
                if p + 1 < PAIRS:
                    self._add_maxima(p + 1, self.max_halves(i))
                if i == 0 and self.early <= p + 2 < PAIRS:
                    self._add(("Q", p + 2), X)
                if i == 1 and self.early <= p + 2 < PAIRS:
                    self._add(("V", p + 2), X)
                if p + 1 < PAIRS and i == nt - 2:
                    self._add(("MT", p + 1), X)
                if p and i == nt - 2:
                    self._add(("RB", p - 1), X)
            self._add(("O", p), O)
        self._add(("MEAN",), X)
        self._add(("DEN", PAIRS - 1), X)
        self._add(("RB", PAIRS - 1), X)
        for g in range(self.out_pairs):
            self._add(("W", g), g % 2)
        self.adds = nt - 1 if self.n_p > 1 else nt

    def _add(self, key, slot):
        self.use[key] = (slot, self.count[slot])
        self.maxima_before[key] = self.count[XB]
        self.count[slot] += 1

    def _add_maxima(self, p, halves):
        for h in halves:
            self._add(("M", p, h), (X, XB)[h % 2])

    def max_halves(self, i):
        n, steps = 2 * self.nt, self.nt - 2
        return range(2 * (n * i // steps), 2 * (n * (i + 1) // steps)) if i < steps else range(0)

    def slot(self, key):
        return self.use[key][0]

    def before(self, b, key):
        return b * self.count[self.use[key][0]] + self.use[key][1]

    def after(self, b, key):
        return self.before(b, key) + 1

    def rounds(self, p, i):
        first, per_pair, last, before_norm = ROUNDS
        start = first + per_pair * p
        if p < 0:
            return range(first)
        if p == PAIRS:
            every = (TAPS + 1) * (TT // 2)
            return range(start - per_pair + last + before_norm if i == 0 else every - LATE[i - 1],
                         every - (LATE[i] if i < len(LATE) else 0))
        if p < PAIRS - 1:
            steps = (1, self.nt - 2, self.nt - 1) if p else (self.nt - 2, self.nt - 1)
            if i not in steps:
                return range(0)
            n = steps.index(i)
            return range(start + per_pair * n // len(steps), start + per_pair * (n + 1) // len(steps))
        if i == self.nt:
            return range(start + last, start + last + before_norm)
        return range(start + last * i // self.nt, start + last * (i + 1) // self.nt)

    def read(self, b, step):
        if step < 0:
            if isinstance(b, int) and b == 0:
                return 0
            return self.read(b, step + PAIRS * self.nt) - PAIRS * self.adds
        p, i = divmod(step, self.nt)
        return b * PAIRS * self.adds + p * self.adds + (max(i, 1) if self.n_p > 1 else i + 1)

    def filled(self, b, key):
        slot, n = self.use[key]
        return b * (self.early_o + PAIRS * self.nt) + n + 1 if slot == O else self.after(b, key)

    def contexts(self, b, step):
        return b * (self.early_o + PAIRS * self.nt) + (self.early_o if step >= 0 else 0) + step + 1

    def ab_value(self, b, p):
        return 16 * 2 * (b * (PAIRS // self.n_ab) + p // self.n_ab + 1)

    def cd_value(self, b, p):
        return 16 * 2 * (b * (PAIRS // self.n_cd) + p // self.n_cd + 1)

    def max_value(self, b, p):
        return 16 * 2 * (b * (PAIRS // self.n_cd) + p // self.n_cd + 1)

    def out_value(self, b, g):
        per_batch = (self.out_pairs + self.n_out - g % self.n_out) // self.n_out
        return 16 * (b * per_batch + g // self.n_out + 1)

    def x1_value(self, c, k):
        return 16 * (c * (TT // 2 // self.n_x1) + k // self.n_x1 + 1)

    y_value = x1_value

    def last_out(self):
        return range(self.out_pairs + 1 - self.n_out, self.out_pairs + 1)


def wait(eng, sem, value):
    if not isinstance(value, int) or value > 0:
        eng.wait_ge(sem, value)


def batches(eng, body):
    body(0)
    body(1)
    with eng.Fori(2, B - 1) as b:
        body(b)
    body(B - 1)


def has_before(b):
    return not isinstance(b, int) or b > 0


def has_two_before(b):
    return not isinstance(b, int) or b > 1


def has_after(b):
    return not isinstance(b, int) or b < B - 1


def f32(ap):
    return ap.bitcast(F32)


def setup(nc, m):
    with ExitStack() as ctx:
        def sb(name, shape, dt=F32):
            return ctx.enter_context(nc.sbuf_tensor(name, shape, dt))

        def sem(name):
            return ctx.enter_context(nc.semaphore(name))

        wq_t, wo_t, wq_e = (sb(n, [P, DC, D]) for n in ("wq_t", "wo_t", "wq_e"))
        before = sb("before", [P, P])
        ones = sb("ones", [P, P])
        token_f, batch_at = sb("token_f", [P, B, TT]), sb("batch_at", [P, B, TT])
        batch_i = sb("batch_i", [P, B, TT], I32)
        order_i, order_f = sb("order_i", [B, T], I32), sb("order_f", [B, T])
        tail = sb("tail", [B, T])
        tile_sums, tile_base = sb("tile_sums", [P, B]), sb("tile_base", [P, B, TT])
        rank, place, spare = (sb(n, [P, B, TT]) for n in ("rank", "place", "spare"))
        n_valid, n_valid_row = sb("n_valid", [P, B]), sb("n_valid_row", [B, 1])
        most = sb("most", [P, 1])
        row_i = sb("row_i", [P, B, TT], I32)

        mask_in, weights_in, stored = sem("mask_in"), sem("weights_in"), sem("stored")
        iotas, blank, shapes_ready = sem("iotas"), sem("blank"), sem("shapes_ready")
        sums_ready, counted, chain, indices = sem("sums_ready"), sem("counted"), sem("chain"), sem("indices")
        high, mean_full, mean_out = sem("weights_high"), sem("mean_full"), sem("mean_out")
        mask3 = m.mask[:].rearrange("p (b j) -> p b j", b=B)
        prefix, totals = m.psum[S0][:, 0, 0:B * TT], m.psum[S0][:, 1, 0:B * TT]
        valid_all, valid_col = m.psum[X][:, 0, 0:B], m.psum[X][0:B, 1, 0:2]
        block = ctx.enter_context(nc.Block())

        @block.sync
        def _(sp):
            sp.dma_start(m.mask[:], m.maskT).then_inc(mask_in, 16)
            for dst, w in ((wq_t, m.wqT), (wo_t, m.woT), (wq_e, m.wq)):
                sp.dma_start(dst[:], w.rearrange("(c p) n -> p c n", p=P)).then_inc(weights_in, 16)
            sp.wait_ge(indices, 3)
            sp.dma_start(m.row_of.rearrange("b p j -> p b j"), row_i[:]).then_inc(stored, 16)
            sp.dma_start(m.tail_rows, tail[:]).then_inc(stored, 16)
            sp.wait_ge(stored, 32)

        @block.gpsimd
        def _(pool):
            nc.gpsimd.iota(m.token[:], [[T, B], [P, TT]], base=0, channel_multiplier=1).then_inc(iotas, 1)
            nc.gpsimd.iota(batch_i[:], [[T, B], [0, TT]], base=0, channel_multiplier=0).then_inc(iotas, 1)
            nc.gpsimd.iota(order_i[:], [[1, T]], base=0, channel_multiplier=0).then_inc(iotas, 1)
            nc.gpsimd.memset(ones[:], 1.0).then_inc(blank, 1)
            nc.gpsimd.memset(m.ident[:], 0.0).then_inc(blank, 1)
            nc.gpsimd.memset(m.one_column[:], 0.0).then_inc(blank, 1)
            pool.wait_ge(blank, 3)
            nc.gpsimd.affine_select(out=m.one_column[:], in_=m.one_column[:], compare_op=ALU.not_equal, fill=1.0,
                                    base=1 - 2 * TT, pattern=[[1, 4 * TT - 1]],
                                    channel_multiplier=0).then_inc(shapes_ready, 1)
            nc.gpsimd.affine_select(out=m.ident[:], in_=m.ident[:], compare_op=ALU.not_equal, fill=1.0, base=0,
                                    pattern=[[-1, P]], channel_multiplier=1).then_inc(shapes_ready, 1)
            nc.gpsimd.affine_select(out=before[:], in_=ones[:], compare_op=ALU.is_ge, fill=0.0, base=-1,
                                    pattern=[[1, P]], channel_multiplier=-1).then_inc(shapes_ready, 1)
            pool.wait_ge(indices, 1)
            for j in range(TT):
                scatter_tokens(nc, m, m.place_i[:, 0, :], m.token[:, 0, :], j)
            pool.wait_ge(m.scattered, 16 * TT)

        @block.tensor
        def _(pe):
            pe.wait_ge(mask_in, 16)
            pe.wait_ge(shapes_ready, 3)
            pe.wait_ge(sums_ready, 1)
            nc.tensor.matmul(prefix, before[:], m.mask[:], start=True, stop=True)
            nc.tensor.matmul(totals, ones[:], m.mask[:], start=True, stop=True)
            nc.tensor.matmul(valid_all, ones[:], tile_sums[:], start=True, stop=True)
            nc.tensor.matmul(valid_col, tile_sums[:], ones[:, 0:2], start=True, stop=True).then_inc(counted, 1)
            pe.wait_ge(weights_in, 48)
            for g in range(DC):
                for c in range(DC):
                    last = nc.tensor.matmul(m.psum[(S1, O)[g // 2]][:, g % 2, :], wq_e[:, c, g * P:(g + 1) * P],
                                            wo_t[:, c, :], start=c == 0, stop=c == DC - 1)
                last.then_inc(mean_full, 1)

        @block.scalar
        def _(act):
            act.wait_ge(shapes_ready, 2)
            nc.scalar.activation(m.ident_r[:], m.ident[:], ACT.Copy).then_inc(high, 1)
            act.wait_ge(weights_in, 48)
            nc.scalar.activation(m.wq_hi[:], wq_t[:], ACT.Copy).then_inc(high, 1)
            nc.scalar.activation(m.wo_hi[:], wo_t[:], ACT.Copy).then_inc(high, 1)
            for g in range(DC):
                act.wait_ge(mean_full, g + 1)
                nc.scalar.activation(m.w_mean[:, g, :], m.psum[(S1, O)[g // 2]][:, g % 2, :],
                                     ACT.Copy).then_inc(mean_out, 1)
            act.wait_ge(mean_out, DC)

        @block.vector
        def _(dve):
            done = [0]

            def link(ins):
                done[0] += 1
                ins.then_inc(chain, 1)
                dve.wait_ge(chain, done[0])

            dve.wait_ge(mask_in, 16)
            nc.vector.tensor_reduce(tile_sums[:], mask3, AX.X, ALU.add).then_inc(sums_ready, 1)
            nc.vector.tensor_scalar(m.last_tap[:], m.mask[:, (TAPS - 1) * TT:TAPS * TT], 1.0, None, ALU.add)
            dve.wait_ge(iotas, 3)
            nc.vector.tensor_copy(token_f[:], m.token[:])
            nc.vector.tensor_copy(batch_at[:], batch_i[:])
            nc.vector.tensor_copy(order_f[:], order_i[:])
            link(nc.vector.memset(tile_base[:], 0.0))
            dve.wait_ge(counted, 1)
            tot3 = totals.rearrange("p (b j) -> p b j", b=B)
            for j in range(1, TT):
                link(nc.vector.tensor_tensor(tile_base[:, :, j], tile_base[:, :, j - 1], tot3[:, :, j - 1], ALU.add))
            nc.vector.tensor_copy(n_valid[:], valid_all)
            nc.vector.tensor_copy(n_valid_row[:], valid_col[:, 0:1])
            link(nc.vector.tensor_tensor(rank[:], tile_base[:], prefix.rearrange("p (b j) -> p b j", b=B), ALU.add))
            link(nc.vector.tensor_tensor(spare[:], token_f[:], rank[:], ALU.subtract))
            for b in range(B):
                last = nc.vector.tensor_scalar(spare[:, b, :], spare[:, b, :], n_valid[:, b:b + 1], None, ALU.add)
            link(last)
            link(nc.vector.tensor_tensor(place[:], rank[:], batch_at[:], ALU.add))
            link(nc.vector.tensor_tensor(place[:], place[:], spare[:], ALU.subtract))
            link(nc.vector.tensor_tensor(place[:], place[:], mask3, ALU.mult))
            link(nc.vector.tensor_tensor(place[:], place[:], spare[:], ALU.add))
            nc.vector.tensor_copy(m.place_i[:], place[:]).then_inc(indices, 1)
            link(nc.vector.tensor_scalar(rank[:], rank[:], 1.0, None, ALU.add))
            link(nc.vector.tensor_tensor(rank[:], rank[:], mask3, ALU.mult))
            nc.vector.tensor_copy(row_i[:], rank[:]).then_inc(indices, 1)
            nc.vector.tensor_scalar(tail[:], order_f[:], n_valid_row[:], NEG, ALU.is_ge, ALU.mult).then_inc(indices, 1)
            for b in range(B):
                nc.vector.tensor_scalar(m.valid[:, b, :], token_f[:, 0, :], n_valid[:, b:b + 1], None, ALU.is_lt)
            link(nc.vector.tensor_reduce(most[:], n_valid[:], AX.X, ALU.max))
            nc.vector.tensor_copy(m.most_valid[:], most[:])
            dve.wait_ge(high, 3)
            nc.vector.tensor_tensor(m.wq_lo[:], wq_t[:], f32(m.wq_hi[:]), ALU.subtract)
            link(nc.vector.tensor_tensor(m.wo_lo[:], wo_t[:], f32(m.wo_hi[:]), ALU.subtract))


def scatter_tokens(nc, m, place, token, j):
    nc.gpsimd.indirect_dma_start(m.token_at, bass.IndirectOffsetOnAxis(ap=place[:, j:j + 1], axis=0),
                                 token[:, j:j + 1], None).then_inc(m.scattered, 16)


def path_memory(nc, m, plan):
    n = Memory()
    cap, nt = plan.cap, plan.nt
    with ExitStack() as ctx:
        def sb(name, shape, dt=F32):
            return ctx.enter_context(nc.sbuf_tensor(f"{name}_{cap}", shape, dt))

        n.packed_out = nc.dram_tensor(f"packed_out_{cap}", [1 + cap, D], F32, kind="Internal").ap()
        n.token_idx = sb("token_idx", [P, nt], I32)
        n.row_idx = sb("row_idx", [P, TT], I32)
        n.xg = sb("xg", [P, nt, D])
        n.xt_hi, n.xt_lo = sb("xt_hi", [P, DC, cap], F32R), sb("xt_lo", [P, DC, cap], F32R)
        n.q_parts = sb("q_parts", [P, plan.n_hl, 2, cap], F32R)
        n.q_lo, n.q_hi = n.q_parts[:, :, 0, :], n.q_parts[:, :, 1, :]
        n.ab = sb("ab", [P, plan.n_ab, 2, 2, cap], F32R)
        n.cd = sb("cd", [P, plan.n_cd, 2, 2, cap], F32R)
        n.prob = sb("prob", [P, plan.n_p, 2, cap])
        n.prob_sum = sb("prob_sum", [P, plan.n_ps, 2, cap])
        n.v = sb("v", [P, PAIRS, cap])
        n.neg_max = sb("neg_max", [P, 2, 2, 2 * nt])
        n.neg_row = sb("neg_row", [P, 2, 2 * nt])
        n.max_row = sb("max_row", [2 * nt, plan.n_cd, P], F32R)
        n.raw = sb("raw", [P, plan.n_raw, cap])
        n.recip = sb("recip", [P, P])
        n.out_st = sb("out_st", [P, plan.n_out, 2, D])
        n.xbar = sb("xbar", [P, DC])
        n.x1 = sb("x1", [P, plan.n_x1, 2, PAD + D])
        n.g = sb("g", [P, 2, D])
        n.y = sb("y", [P, plan.n_x1, 2, D])
        n.xm = n.out_st[:, 0].rearrange("p a c -> p (a c)")
        n.place_now, n.token_now = sb("place_now", [P, TT], I32), sb("token_now", [P, TT], I32)
        n.valid_now = sb("valid_now", [P, TT])
    return n


def halves(ap, plan):
    return ap.rearrange("p (a c) -> p a c", a=2)


CONV_PAIR = 2 * (TAPS + 1)
CONV_BATCH = CONV_PAIR * (TT // 2)


def tensor_program(nc, pe, m, r, plan):
    nt, cap, half = plan.nt, plan.cap, plan.half

    def claim(b, key):
        wait(pe, m.free[plan.slot(key)], plan.before(b, key))
        if plan.slot(key) == X and key[0] in ("T", "Q", "V", "RB"):
            wait(pe, m.free[XB], b * plan.count[XB] + plan.maxima_before[key])
        return m.psum[X if plan.slot(key) == XB else plan.slot(key)]

    def filled(ins, key):
        ins.then_inc(m.full[plan.slot(key)], 1)

    def project(b, p, halves=(), first=2):
        q = claim(b, ("Q", p))
        done = 0
        for a in range(2):
            n = 0
            for c in range(DC):
                if p == 0 and a == 0:
                    pe.wait_ge(m.free[plan.slot(("T", c))], plan.after(b, ("T", c)))
                for w, xt in ((m.wq_hi, r.xt_hi), (m.wq_lo, r.xt_hi), (m.wq_hi, r.xt_lo)):
                    last = nc.tensor.matmul(q[:, a, 0:half], w[:, c, p * P:(p + 1) * P],
                                            xt[:, c, a * half:(a + 1) * half], start=n == 0, stop=n == 3 * DC - 1)
                    n += 1
                    if a * 3 * DC + n >= first and n % 2 == 0:
                        maxima(b, 0, halves[done:done + 1])
                        done += 1
        filled(last, ("Q", p))
        maxima(b, 0, halves[done:])

    def values(b, p):
        v = claim(b, ("V", p)).rearrange("p a c -> p (a c)")
        pe.wait_ge(m.free[plan.slot(("Q", p))], plan.after(b, ("Q", p)))
        for i in range(nt):
            for n, q in enumerate((r.q_hi, r.q_lo)):
                last = nc.tensor.matmul(v[:, i * P:(i + 1) * P], q[:, p % plan.n_hl, i * P:(i + 1) * P], m.ident_r[:],
                                        start=n == 0, stop=n == 1)
        filled(last, ("V", p))

    def maxima(b, p, halves):
        ab = r.ab[:, p % plan.n_ab]
        for h in halves:
            hh, i, a = h // 2 // nt, h // 2 % nt, h % 2
            s = claim(b, ("M", p, h))
            if h % (2 * nt) == 0:
                pe.wait_ge(m.ab_in[p % plan.n_ab][hh], plan.ab_value(b, p))
            filled(nc.tensor.matmul(s[:, a, 0:half], ab[:, hh, 0, i * P:(i + 1) * P],
                                    ab[:, hh, 1, a * half:(a + 1) * half], start=True, stop=True), ("M", p, h))

    def portion(halves, n, late):
        skipped = 2 if late else 0
        k, of = n - skipped, 6 - skipped
        return halves[len(halves) * k // of:len(halves) * (k + 1) // of] if k >= 0 else halves[:0]

    def max_transpose(b, p):
        key = ("MT", p)
        s = claim(b, key)
        pe.wait_ge(m.maxima_taken, b * PAIRS + p + 1)
        filled(nc.tensor.transpose(s[0:2 * nt, 0, 0:P], r.neg_row[:, p % 2, :], m.ident[:]), key)

    def denominators(b, p):
        s = claim(b, ("DEN", p))
        for hh in range(2):
            pe.wait_ge(m.added[hh], (b * PAIRS + p + 1) * plan.adds)
        for t in range(2 * nt):
            hh, i = divmod(t, nt)
            last = nc.tensor.matmul(s[0:2 * nt, 0, 0:P], m.one_column[:, 2 * TT - 1 - t:2 * TT - 1 - t + 2 * nt],
                                    r.prob_sum[:, p % plan.n_ps, hh, i * P:(i + 1) * P],
                                    start=t == 0, stop=t == 2 * nt - 1)
        filled(last, ("DEN", p))

    def spread(b, p):
        s = claim(b, ("RB", p)).rearrange("p a c -> p (a c)")
        pe.wait_ge(m.recips, b * PAIRS + p + 1)
        for i in range(nt):
            for hh in range(2):
                row = m.ident[:, hh * nt + i:hh * nt + i + 1].to_broadcast([P, DK])
                last = nc.tensor.matmul(s[hh * DK:(hh + 1) * DK, i * P:(i + 1) * P], row, r.recip[:],
                                        start=True, stop=True)
        filled(last, ("RB", p))

    def context(b, p, i, a):
        if i == 0 and a == 0:
            claim(b, ("O", p))
            if plan.slot(("V", p)) == X:
                pe.wait_ge(m.free[X], plan.after(b, ("V", p)))
        if a == 0:
            for hh in range(2):
                pe.wait_ge(m.free[hh], plan.after(b, ("S", p, i, hh)))
        step = p * nt + i
        for hh in range(2):
            last = nc.tensor.matmul(m.psum[O][hh * DK:(hh + 1) * DK, a, 0:half],
                                    r.v[:, p, i * P + hh * DK:i * P + (hh + 1) * DK],
                                    r.prob[:, step % plan.n_p, hh, a * half:(a + 1) * half],
                                    start=i == 0, stop=i == nt - 1)
        if a == 1:
            last.then_inc(m.full[O], 1)

    def output_rows(b, g, pairs):
        w = claim(b, ("W", g)) if pairs[0] == 0 else m.psum[g % 2]
        for a in range(min(2, nt - 2 * g)):
            i = 2 * g + a
            for c in pairs:
                for n, (ct, wo) in enumerate(((r.xt_hi, m.wo_hi), (r.xt_lo, m.wo_hi), (r.xt_hi, m.wo_lo))):
                    last = nc.tensor.matmul(w[:, a, :], ct[:, c, i * P:(i + 1) * P], wo[:, c, :],
                                            start=c == 0 and n == 0, stop=c == PAIRS - 1 and n == 2)
        if pairs[-1] == PAIRS - 1:
            filled(last, ("W", g))

    def transposes(b, groups):
        pe.wait_ge(m.rows_masked, (b + 1) * nt)
        for c in groups:
            s = claim(b, ("T", c)).rearrange("p a c -> p (a c)")
            for i in range(nt):
                last = nc.tensor.transpose(s[:, i * P:(i + 1) * P], r.xg[:, i, c * P:(c + 1) * P], m.ident[:])
            filled(last, ("T", c))

    def mean_row(b):
        s = claim(b, ("MEAN",))
        pe.wait_ge(m.channel_mean, (b + 1) * DC)
        for c in range(DC):
            last = nc.tensor.matmul(s[0:1, 0, :], r.xbar[:, c:c + 1], m.w_mean[:, c, :],
                                    start=c == 0, stop=c == DC - 1)
        filled(last, ("MEAN",))

    def body(b):
        if not has_before(b):
            transposes(0, range(2))
        transposes(b, range(2, DC))
        project(b, 0)
        project(b, 1)
        values(b, 0)
        if plan.early == PAIRS:
            project(b, 2, range(2 * nt), DC * 3)
            values(b, 1)
            project(b, 3, range(2 * nt, 4 * nt))
            max_transpose(b, 0)
            values(b, 2)
            values(b, 3)
        else:
            maxima(b, 0, range(4 * nt))
            values(b, 1)
            max_transpose(b, 0)
        previous = None
        for p in range(PAIRS):
            ab, cd = r.ab[:, p % plan.n_ab], r.cd[:, p % plan.n_cd]
            for i in range(nt):
                if i == 0:
                    if p == 0:
                        pe.wait_ge(m.tails_in, 16 * (b + 1))
                    pe.wait_ge(m.cd_in[p % plan.n_cd], plan.cd_value(b, p))
                    pe.wait_ge(m.max_in[p % plan.n_cd], plan.max_value(b, p))
                halves = plan.max_halves(i) if p + 1 < PAIRS else range(0)
                for hh in range(2):
                    s = claim(b, ("S", p, i, hh))
                    for a in range(2):
                        cols = slice(a * half, (a + 1) * half)
                        nc.tensor.matmul(s[:, a, 0:half], ab[:, hh, 0, i * P:(i + 1) * P], ab[:, hh, 1, cols],
                                         start=True, stop=False)
                        last = nc.tensor.matmul(s[:, a, 0:half], cd[:, hh, 1, i * P:(i + 1) * P],
                                                cd[:, hh, 0, cols], start=False, stop=True)
                        if a == 1:
                            filled(last, ("S", p, i, hh))
                        maxima(b, p + 1, portion(halves, 2 * hh + a, p and i == plan.den_step))
                    if hh == 0 and p and i == plan.den_step:
                        denominators(b, p - 1)
                    if hh == 0 and p + 1 < PAIRS and i == nt - 2:
                        max_transpose(b, p + 1)
                for a in range(2):
                    if previous:
                        context(b, *previous, a)
                    maxima(b, p + 1, portion(halves, 4 + a, p and i == plan.den_step))
                previous = (p, i)
                if i == 0 and plan.early <= p + 2 < PAIRS:
                    project(b, p + 2)
                if i == 1 and plan.early <= p + 2 < PAIRS:
                    values(b, p + 2)
                if p and i == nt - 2:
                    spread(b, p - 1)
        for a in range(2):
            context(b, *previous, a)
        mean_row(b)
        denominators(b, PAIRS - 1)
        pe.wait_ge(m.ctx_split, b * PAIRS + PAIRS - 1)
        output_rows(b, 0, range(PAIRS - 1))
        spread(b, PAIRS - 1)
        output_rows(b, 1, range(PAIRS - 1))
        if has_after(b):
            transposes(b + 1, range(2))
        pe.wait_ge(m.ctx_split, (b + 1) * PAIRS)
        for g in range(plan.out_pairs):
            output_rows(b, g, range(PAIRS - 1, PAIRS) if g < 2 else range(PAIRS))

    batches(pe, body)


def scalar_program(nc, act, m, r, plan):
    nt, cap, half = plan.nt, plan.cap, plan.half

    def ready(b, key):
        act.wait_ge(m.full[plan.slot(key)], plan.filled(b, key))
        return m.psum[plan.slot(key)]

    def drained(ins, key):
        ins.then_inc(m.free[plan.slot(key)], 1)

    def mask_rows(b, i):
        if i == 0:
            act.wait_ge(m.rows_in, 16 * nt * (b + 1))
            act.wait_ge(m.valid_ready, 3 * b + 1)
        nc.scalar.activation(r.xg[:, i, :], r.xg[:, i, :], ACT.Copy,
                             scale=r.valid_now[:, i:i + 1]).then_inc(m.rows_masked, 1)

    def high_of_projection(b, p):
        s = ready(b, ("Q", p))
        if p >= plan.n_hl:
            for hh in range(2):
                act.wait_ge(m.ab_in[(p - plan.n_hl) % plan.n_ab][hh], plan.ab_value(b, p - plan.n_hl))
            act.wait_ge(m.cd_in[(p - plan.n_hl) % plan.n_cd], plan.cd_value(b, p - plan.n_hl))
        elif has_before(b):
            old = p - plan.n_hl + PAIRS
            for hh in range(2):
                act.wait_ge(m.ab_in[old % plan.n_ab][hh], plan.ab_value(b - 1, old))
            act.wait_ge(m.cd_in[old % plan.n_cd], plan.cd_value(b - 1, old))
        nc.scalar.activation(halves(r.q_hi[:, p % plan.n_hl, :], plan), s[:, :, 0:half],
                             ACT.Copy).then_inc(m.high, 1)

    def copy_values(b, p):
        s = ready(b, ("V", p)).rearrange("p a c -> p (a c)")
        drained(nc.scalar.activation(r.v[:, p, :], s[:, 0:cap], ACT.Copy), ("V", p))

    def max_row(b, p):
        s = ready(b, ("MT", p))
        wait(act, m.max_in[p % plan.n_cd], plan.max_value(b, p) - 32)
        drained(nc.scalar.activation(r.max_row[:, p % plan.n_cd, :], s[0:2 * nt, 0, 0:P], ACT.Copy), ("MT", p))

    def body(b):
        if not has_before(b):
            for i in range(nt):
                mask_rows(0, i)
        for c in range(DC):
            if has_before(b):
                if c == 0:
                    act.wait_ge(m.full[plan.slot(last_rows)], plan.filled(b - 1, last_rows))
                if c == 2:
                    copy_rows(b - 1, plan.out_pairs - 1)
            s = ready(b, ("T", c)).rearrange("p a c -> p (a c)")
            nc.scalar.activation(r.xt_hi[:, c, :], s[:, 0:cap], ACT.Copy).then_inc(m.high, 1)
        high_of_projection(b, 0)
        high_of_projection(b, 1)
        copy_values(b, 0)
        if plan.early == PAIRS:
            high_of_projection(b, 2)
            copy_values(b, 1)
            high_of_projection(b, 3)
            max_row(b, 0)
            copy_values(b, 2)
            copy_values(b, 3)
        else:
            copy_values(b, 1)
            max_row(b, 0)
        for p in range(PAIRS):
            for i in range(nt):
                step = p * nt + i
                for hh in range(2):
                    s = ready(b, ("S", p, i, hh))
                    if has_before(b) or step >= plan.n_p:
                        act.wait_ge(m.full[O], plan.contexts(b, step - plan.n_p))
                    wait(act, m.added[hh], plan.read(b, step - plan.n_p))
                    drained(nc.scalar.activation(halves(r.prob[:, step % plan.n_p, hh, :], plan),
                                                 s[:, :, 0:half], ACT.Exp, scale=SCALE), ("S", p, i, hh))
                    if hh == 0 and i == nt - 2 and p + 1 < PAIRS:
                        max_row(b, p + 1)
                if i == 0 and p:
                    raw_context(b, p - 1)
                if i == 0 and plan.early <= p + 2 < PAIRS:
                    high_of_projection(b, p + 2)
                if i == 1 and plan.early <= p + 2 < PAIRS:
                    copy_values(b, p + 2)
                if p and i == nt - 1:
                    high_of_context(b, p - 1)
                if i == 1:
                    channel_mean(b, p)
                if p == PAIRS - 1 and has_after(b):
                    mask_rows(b + 1, i)
        raw_context(b, PAIRS - 1)
        s = ready(b, ("MEAN",))
        wait(act, m.out_stored[0], plan.out_value(b, 0) - 16)
        drained(nc.scalar.activation(r.out_st[0:1, 0, 0, :], s[0:1, 0, :], ACT.Copy), ("MEAN",))
        high_of_context(b, PAIRS - 1)
        for g in range(plan.out_pairs - (1 if has_after(b) else 0)):
            copy_rows(b, g)

    last_rows = ("W", plan.out_pairs - 1)

    def copy_rows(b, g):
        s = ready(b, ("W", g))
        buf, tiles = (g + 1) % plan.n_out, min(2, nt - 2 * g)
        wait(act, m.out_stored[buf], plan.out_value(b, g + 1) - 16)
        drained(nc.scalar.activation(r.out_st[:, buf, 0:tiles, :], s[:, 0:tiles, :], ACT.Copy), ("W", g))

    def raw_context(b, p):
        act.wait_ge(m.full[O], plan.contexts(b, p * nt + nt - 1))
        wait(act, m.ctx_split, b * PAIRS + p - plan.n_raw + 1)
        nc.scalar.activation(halves(r.raw[:, p % plan.n_raw, :], plan), m.psum[O][:, :, 0:half],
                             ACT.Copy).then_inc(m.free[O], 1)

    def high_of_context(b, p):
        act.wait_ge(m.free[X], plan.after(b, ("RB", p)))
        nc.scalar.activation(r.xt_hi[:, p, :], r.raw[:, p % plan.n_raw, :], ACT.Copy).then_inc(m.high, 1)

    def channel_mean(b, c):
        act.wait_ge(m.xm_in, 16 * (b * DC + c + 1))
        nc.scalar.activation(r.xm, r.xm, ACT.Copy, scale=1.0 / T,
                             accum_out=r.xbar[:, c:c + 1]).then_inc(m.channel_mean, 1)

    batches(act, body)


def vector_program(nc, dve, m, r, plan):
    nt, cap, half = plan.nt, plan.cap, plan.half

    def ready(b, key):
        dve.wait_ge(m.full[plan.slot(key)], plan.filled(b, key))
        return m.psum[plan.slot(key)]

    def drained(ins, key):
        ins.then_inc(m.free[plan.slot(key)], 1)

    def low_of_projection(b, p):
        s = ready(b, ("Q", p))
        dve.wait_ge(m.high, b * (DC + 2 * PAIRS) + DC + p + 1)
        drained(nc.vector.tensor_tensor(halves(r.q_lo[:, p % plan.n_hl, :], plan), s[:, :, 0:half],
                                        halves(f32(r.q_hi[:, p % plan.n_hl, :]), plan), ALU.subtract), ("Q", p))

    def maxima(b, p, halves):
        for h in halves:
            t, a = divmod(h, 2)
            dve.wait_ge(m.full[(X, XB)[a]], plan.after(b, ("M", p, h)))
            drained(nc.vector.tensor_reduce(r.neg_max[:, p % 2, a, t:t + 1], m.psum[X][:, a, 0:half], AX.X,
                                            ALU.max, negate=True), ("M", p, h))
        if len(halves) and halves[-1] == 4 * nt - 1:
            dve.wait_ge(m.free[XB], plan.after(b, ("M", p, 4 * nt - 1)))
            nc.vector.tensor_tensor(r.neg_row[:, p % 2, :], r.neg_max[:, p % 2, 0, :], r.neg_max[:, p % 2, 1, :],
                                    ALU.min).then_inc(m.maxima_taken, 1)

    def reciprocals(b, p):
        s = ready(b, ("DEN", p))
        drained(nc.vector.tensor_scalar(r.recip[0:2 * nt, :], s[0:2 * nt, 0, 0:P], 1e-30, None, ALU.max), ("DEN", p))
        dve.wait_ge(m.free[X], plan.after(b, ("DEN", p)))
        nc.vector.reciprocal(r.recip[0:2 * nt, :], r.recip[0:2 * nt, :]).then_inc(m.recips, 1)

    def normalise(b, p):
        s = ready(b, ("RB", p)).rearrange("p a c -> p (a c)")
        dve.wait_ge(m.free[O], plan.after(b, ("O", p)))
        raw = r.raw[:, p % plan.n_raw, :]
        drained(nc.vector.tensor_tensor(raw, raw, s[:, 0:cap], ALU.mult), ("RB", p))

    def low_of_context(b, p):
        dve.wait_ge(m.high, b * (DC + 2 * PAIRS) + DC + PAIRS + p + 1)
        nc.vector.tensor_tensor(r.xt_lo[:, p, :], r.raw[:, p % plan.n_raw, :], f32(r.xt_hi[:, p, :]),
                                ALU.subtract).then_inc(m.ctx_split, 1)

    def conv_round(c, n):
        k, step = divmod(n, TAPS + 1)
        x1, y = r.x1[:, k % plan.n_x1], r.y[:, k % plan.n_x1]
        done = c * CONV_BATCH + k * CONV_PAIR
        if step == 0:
            dve.wait_ge(m.x1_in[k % plan.n_x1], plan.x1_value(c, k))
            dve.wait_ge(m.g_in, 32 * (c * (TT // 2) + k + 1))
        if step == 1:
            wait(dve, m.y_stored[k % plan.n_x1], plan.y_value(c, k) - 16)
        for u in range(2):
            if step:
                dve.wait_ge(m.conv, done + 2 * step - 1 + u)
            if step == 0:
                ins = nc.vector.tensor_tensor(x1[:, u, PAD:PAD + D], x1[:, u, PAD:PAD + D], r.g[:, u, :], ALU.add)
            elif step == 1:
                ins = nc.vector.tensor_scalar(y[:, u, :], x1[:, u, PAD:PAD + D],
                                              m.last_tap[:, 2 * k + u:2 * k + u + 1], None, ALU.mult)
            else:
                tap = step - 2
                j = tap * TT + 2 * k + u
                ins = nc.vector.scalar_tensor_tensor(y[:, u, :], x1[:, u, tap:tap + D], m.mask[:, j:j + 1],
                                                     y[:, u, :], ALU.mult, ALU.add)
            ins.then_inc(m.conv, 1)

    def body(b):
        if isinstance(b, int) and b == 0:
            nc.vector.memset(r.x1[:], 0.0).then_inc(m.zeroed, 1)
            nc.vector.memset(r.recip[:], 0.0).then_inc(m.zeroed, 1)
            for n in range(plan.n_cd):
                for hh in range(2):
                    nc.vector.memset(f32(r.cd[DK:P, n, hh, 1, :]), 0.0).then_inc(m.zeroed, 1)
                    nc.vector.memset(f32(r.cd[DK:P, n, hh, 0, :]), 1.0).then_inc(m.zeroed, 1)
            dve.wait_ge(m.zeroed, 2 + 4 * plan.n_cd)
            for n in range(plan.n_cd):
                for hh in range(2):
                    nc.vector.memset(f32(r.cd[DK:DK + 1, n, hh, 1, :]), 1.0).then_inc(m.zeroed, 1)
            nc.vector.tensor_copy(r.valid_now[:], m.valid[:, 0, :]).then_inc(m.valid_ready, 1)
        for c in range(DC):
            s = ready(b, ("T", c)).rearrange("p a c -> p (a c)")
            dve.wait_ge(m.high, b * (DC + 2 * PAIRS) + c + 1)
            drained(nc.vector.tensor_tensor(r.xt_lo[:, c, :], s[:, 0:cap], f32(r.xt_hi[:, c, :]), ALU.subtract),
                    ("T", c))
        if has_after(b):
            nxt = slice(b + 1, b + 2) if isinstance(b, int) else bass.ds(b + 1, 1)
            for now, every in ((r.place_now, m.place_i), (r.token_now, m.token), (r.valid_now, m.valid)):
                last = nc.vector.tensor_copy(now[:], every[:, nxt, :].rearrange("p o j -> p (o j)"))
                last.then_inc(m.valid_ready, 1)
        for p in range(2):
            if has_two_before(b):
                for n in plan.rounds(PAIRS, p + 1):
                    conv_round(b - 2, n)
            low_of_projection(b, p)
        if has_two_before(b):
            for n in plan.rounds(PAIRS, 3):
                conv_round(b - 2, n)
        if plan.early == PAIRS:
            maxima(b, 0, range(2 * nt))
            low_of_projection(b, 2)
            maxima(b, 0, range(2 * nt, 4 * nt))
            low_of_projection(b, 3)
        else:
            maxima(b, 0, range(4 * nt))
        if has_before(b):
            for n in plan.rounds(-1, 0):
                conv_round(b - 1, n)
        for p in range(PAIRS):
            for i in range(nt):
                if p and i == plan.den_step:
                    reciprocals(b, p - 1)
                if p + 1 < PAIRS:
                    maxima(b, p + 1, plan.max_halves(i))
                if i == 0 and plan.early <= p + 2 < PAIRS:
                    low_of_projection(b, p + 2)
                if p == PAIRS - 1 and i == nt - 2:
                    normalise(b, p - 1)
                if has_before(b):
                    for n in plan.rounds(p, i):
                        conv_round(b - 1, n)
                if 0 < p < PAIRS - 1 and i == nt - 2:
                    normalise(b, p - 1)
                if p and i == nt - 1:
                    low_of_context(b, p - 1)
        if has_before(b):
            for n in plan.rounds(PAIRS - 1, nt):
                conv_round(b - 1, n)
        reciprocals(b, PAIRS - 1)
        normalise(b, PAIRS - 1)
        low_of_context(b, PAIRS - 1)
        if has_before(b):
            for step in range(4 if not has_after(b) else 1):
                for n in plan.rounds(PAIRS, step):
                    conv_round(b - 1, n)

    batches(dve, body)
    for n in range((TAPS + 1) * (TT // 2)):
        conv_round(B - 1, n)


def gpsimd_program(nc, pool, m, r, plan):
    nt = plan.nt

    def hold(sem, value):
        if not isinstance(value, int) or value > 0:
            pool.wait_ge(sem, value)
            pool.sem_inc(m.pool_passed, 1)

    def gather_ready(b):
        hold(m.tokens_in, 16 * (b + 1))
        if has_before(b):
            hold(m.full[plan.slot(("T", DC - 1))], plan.filled(b - 1, ("T", DC - 1)))

    def gather_tile(i):
        nc.gpsimd.indirect_dma_start(r.xg[:, i, :], None, m.xT,
                                     bass.IndirectOffsetOnAxis(ap=r.token_idx[:, i:i + 1], axis=0)
                                     ).then_inc(m.rows_in, 16)

    def gather_outputs(c, k):
        if k == 0:
            hold(m.out_rows_in, 16 * (c + 1))
            for g in plan.last_out():
                hold(m.out_stored[g % plan.n_out], plan.out_value(c, g))
        hold(m.conv, c * CONV_BATCH + (CONV_PAIR * (k - 1) + 2 if k else 0))
        for u in range(2):
            nc.gpsimd.indirect_dma_start(r.g[:, u, :], None, r.packed_out,
                                         bass.IndirectOffsetOnAxis(ap=r.row_idx[:, 2 * k + u:2 * k + u + 1], axis=0)
                                         ).then_inc(m.g_in, 16)

    def body(b):
        if isinstance(b, int) and b == 0:
            gather_ready(0)
            for i in range(nt):
                gather_tile(i)
        if has_before(b):
            gather_outputs(b - 1, 0)
        if has_after(b):
            hold(m.valid_ready, 3 * b + 4)
            for j in range(TT):
                scatter_tokens(nc, m, r.place_now, r.token_now, j)
            gather_ready(b + 1)
            for i in range(nt):
                gather_tile(i)
        for p in range(PAIRS):
            for i in range(nt):
                step = p * nt + i
                if i == 0:
                    if p >= plan.n_ps:
                        pool.wait_ge(m.full[X], plan.after(b, ("DEN", p - plan.n_ps)))
                    elif has_before(b):
                        pool.wait_ge(m.full[X], plan.after(b - 1, ("DEN", p - plan.n_ps + PAIRS)))
                for hh in range(2):
                    total = r.prob_sum[:, p % plan.n_ps, hh, :]
                    now = r.prob[:, step % plan.n_p, hh, :]
                    if i or plan.n_p == 1:
                        hold(m.free[hh], plan.after(b, ("S", p, i, hh)))
                    if i == 0:
                        if plan.n_p == 1:
                            nc.gpsimd.tensor_copy(total, now).then_inc(m.added[hh], 1)
                        continue
                    wait(pool, m.added[hh], plan.read(b, step) - 1)
                    first = r.prob[:, (step - 1) % plan.n_p, hh, :] if i == 1 and plan.n_p > 1 else total
                    nc.gpsimd.tensor_tensor(total, first, now, ALU.add).then_inc(m.added[hh], 1)
                if has_before(b) and (p, i) in ((0, 1), (2, nt - 1), (3, nt - 1)):
                    gather_outputs(b - 1, (1, 0, 2, 3)[p])
    batches(pool, body)
    for k in range(TT // 2):
        gather_outputs(B - 1, k)


def sync_program(nc, sp, m, r, plan):
    nt, cap = plan.nt, plan.cap

    def hold(sem, value):
        if not isinstance(value, int) or value > 0:
            sp.wait_ge(sem, value)
            sp.sem_inc(m.sync_passed, 1)

    def tokens(b):
        if has_before(b):
            hold(m.scattered, 16 * TT * (b + 1))
            hold(m.rows_in, 16 * nt * b)
        sp.dma_start(r.token_idx[:], m.token_at3[b].rearrange("(j p) -> p j", p=P)[:, 0:nt],
                     allow_slow_non_contiguous=True).then_inc(m.tokens_in, 16)

    def first_operands(b, p):
        buf = p % plan.n_ab
        hold(m.free[plan.slot(("Q", p))], plan.after(b, ("Q", p)))
        if p >= plan.n_ab:
            hold(m.full[S1], plan.after(b, ("S", p - plan.n_ab, nt - 1, 1)))
        elif has_before(b):
            hold(m.full[S1], plan.after(b - 1, ("S", p - plan.n_ab + PAIRS, nt - 1, 1)))
        for hh in range(2):
            rows = slice(hh * DK, (hh + 1) * DK)
            hi = f32(r.q_hi[rows, p % plan.n_hl, :])
            both = hi.rearrange("p (o c) -> p o c", o=1).to_broadcast([DK, 2, cap])
            sp.dma_start(f32(r.ab[0:DK, buf, hh, :, :]), both).then_inc(m.ab_in[buf][hh], 16)
            sp.dma_start(f32(r.ab[DK:P, buf, hh, :, :]), f32(r.q_parts[rows, p % plan.n_hl, :, :])
                         ).then_inc(m.ab_in[buf][hh], 16)

    def tails(b):
        if has_before(b):
            hold(m.full[S1], plan.after(b - 1, ("S", PAIRS - 1, nt - 1, 1)))
        else:
            hold(m.zeroed, 2 + 6 * plan.n_cd)
        row = m.tail_rows[bass.ds(b, 1), 0:cap].rearrange("o (x c) -> o x c", x=1)
        sp.dma_start(f32(r.cd[DK + 1:DK + 2, :, :, 1, :]).rearrange("o n h c -> o (n h) c"),
                     row.to_broadcast([1, 2 * plan.n_cd, cap])).then_inc(m.tails_in, 16)

    def second_operands(b, p):
        buf = p % plan.n_cd
        hold(m.free[plan.slot(("Q", p))], plan.after(b, ("Q", p)))
        if p >= plan.n_cd:
            hold(m.full[S1], plan.after(b, ("S", p - plan.n_cd, nt - 1, 1)))
        elif has_before(b):
            hold(m.full[S1], plan.after(b - 1, ("S", p - plan.n_cd + PAIRS, nt - 1, 1)))
        for hh in range(2):
            rows = slice(hh * DK, (hh + 1) * DK)
            sp.dma_start(f32(r.cd[0:DK, buf, hh, :, :]), f32(r.q_parts[rows, p % plan.n_hl, :, :])
                         ).then_inc(m.cd_in[buf], 16)

    def max_rows(b, p):
        buf = p % plan.n_cd
        hold(m.free[X], plan.after(b, ("MT", p)))
        for hh in range(2):
            sp.dma_start(f32(r.cd[DK:DK + 1, buf, hh, 0, :]).rearrange("o (i q) -> o i q", i=nt),
                         f32(r.max_row[hh * nt:(hh + 1) * nt, buf, :])).then_inc(m.max_in[buf], 16)

    def conv_load(c, k):
        hold(m.conv, c * CONV_BATCH + (k + 1 - plan.n_x1) * CONV_PAIR if k + 1 >= plan.n_x1 else c * CONV_BATCH)
        if k == 0 and isinstance(c, int) and c == 0:
            hold(m.zeroed, 1)
        sp.dma_start(r.x1[:, k % plan.n_x1, :, PAD:PAD + D], m.xT4[c * (TT // 2) + k]
                     ).then_inc(m.x1_in[k % plan.n_x1], 16)

    def conv_store(c, k):
        hold(m.conv, c * CONV_BATCH + (k + 1) * CONV_PAIR)
        sp.dma_start(m.out4[c * (TT // 2) + k], r.y[:, k % plan.n_x1]).then_inc(m.y_stored[k % plan.n_x1], 16)

    def conv_follow(c, k):
        conv_store(c, k)
        if k + plan.n_x1 < TT // 2:
            conv_load(c, k + plan.n_x1)

    def mean_load(b, c):
        if c == 0 and has_before(b):
            for g in plan.last_out():
                hold(m.out_stored[g % plan.n_out], plan.out_value(b - 1, g))
        hold(m.channel_mean, b * DC + c)
        sp.dma_start(r.xm, m.x4[b * DC + c]).then_inc(m.xm_in, 16)

    def output_rows(c):
        hold(m.g_in, 32 * (TT // 2) * c)
        sp.dma_start(r.row_idx[:], m.row_of[c]).then_inc(m.out_rows_in, 16)

    def body(b):
        if isinstance(b, int) and b == 0:
            tokens(0)
        mean_load(b, 0)
        tails(b)
        first_operands(b, 0)
        second_operands(b, 0)
        if has_before(b):
            output_rows(b - 1)
        if has_two_before(b):
            conv_follow(b - 2, 3)
        first_operands(b, 1)
        if plan.n_cd > 1:
            second_operands(b, 1)
        if has_before(b):
            for k in range(plan.n_x1):
                conv_load(b - 1, k)
        max_rows(b, 0)
        if has_after(b):
            tokens(b + 1)
        for p in range(PAIRS):
            if p < 2:
                if p + 2 < plan.n_ab:
                    first_operands(b, p + 2)
            if p and p + 1 < PAIRS and plan.n_ab <= p + 1:
                first_operands(b, p + 1)
            if p and p + 1 < PAIRS and plan.n_cd > 1:
                second_operands(b, p + 1)
            if p + 1 < DC:
                mean_load(b, p + 1)
            if p + 1 < PAIRS:
                if plan.n_cd == 1:
                    second_operands(b, p + 1)
                max_rows(b, p + 1)
            if has_before(b) and p in (1, 3):
                conv_follow(b - 1, p // 2)
        hold(m.g_in, 32 * (TT // 2) * b)
        hold(m.free[X], plan.after(b, ("MEAN",)))
        sp.dma_start(r.packed_out[0:1, :], r.out_st[0:1, 0, 0, :]).then_inc(m.out_stored[0], 16)
        for g in range(plan.out_pairs):
            hold(m.free[g % 2], plan.after(b, ("W", g)))
            buf, tiles = (g + 1) % plan.n_out, min(2, nt - 2 * g)
            rows = r.packed_out[1 + 2 * g * P:1 + (2 * g + tiles) * P, :]
            sp.dma_start(rows.rearrange("(a p) d -> p a d", p=P), r.out_st[:, buf, 0:tiles, :]
                         ).then_inc(m.out_stored[buf], 16)
        if has_before(b):
            conv_follow(b - 1, 2)
            if not has_after(b):
                conv_follow(b - 1, 3)

    batches(sp, body)
    output_rows(B - 1)
    conv_load(B - 1, 0)
    for k in range(TT // 2):
        if k + 1 < TT // 2 and plan.n_x1 > 1:
            conv_load(B - 1, k + 1)
        conv_store(B - 1, k)
        if k + 1 < TT // 2 and plan.n_x1 == 1:
            conv_load(B - 1, k + 1)
    for k in range(TT // 2 - plan.n_x1, TT // 2):
        hold(m.y_stored[k % plan.n_x1], plan.y_value(B - 1, k))


def cond_attn_conv(nc, xT, x, maskT, wqT, woT, wq, out):
    with ExitStack() as ctx:
        def sb(name, shape, dt=F32):
            return ctx.enter_context(nc.sbuf_tensor(name, shape, dt))

        def sem(name):
            return ctx.enter_context(nc.semaphore(name))

        def sems(name, n):
            return [sem(f"{name}{i}") for i in range(n)]

        m = Memory()
        m.xT, m.maskT, m.wqT, m.woT, m.wq = xT, maskT, wqT, woT, wq
        m.xT4 = xT.rearrange("(n u p) d -> n p u d", p=P, u=2)
        m.x4 = x.rearrange("(n p) t -> n p t", p=P)
        m.out4 = out.rearrange("(n u p) d -> n p u d", p=P, u=2)
        m.token_at = nc.dram_tensor("token_at", [B * T, 1], I32, kind="Internal").ap()
        m.token_at3 = m.token_at.rearrange("(b t) o -> b (t o)", b=B)
        m.row_of = nc.dram_tensor("row_of", [B, P, TT], I32, kind="Internal").ap()
        m.tail_rows = nc.dram_tensor("tail_rows", [B, T], F32, kind="Internal").ap()

        m.mask = sb("mask", [P, B * TT])
        m.wq_hi, m.wq_lo = sb("wq_hi", [P, DC, D], F32R), sb("wq_lo", [P, DC, D], F32R)
        m.wo_hi, m.wo_lo = sb("wo_hi", [P, DC, D], F32R), sb("wo_lo", [P, DC, D], F32R)
        m.w_mean = sb("w_mean", [P, DC, D])
        m.ident, m.ident_r = sb("ident", [P, P]), sb("ident_r", [P, P], F32R)
        m.one_column = sb("one_column", [P, 4 * TT - 1])
        m.valid = sb("valid", [P, B, TT])
        m.last_tap = sb("last_tap", [P, TT])
        m.place_i, m.token = sb("place_i", [P, B, TT], I32), sb("token", [P, B, TT], I32)
        m.most_valid = sb("most_valid", [P, 1], I32)
        m.psum = [ctx.enter_context(nc.psum_tensor(f"slot{n}", [P, 2, BANK], F32)) for n in range(4)]
        m.scattered, m.zeroed, m.valid_ready = sem("scattered"), sem("zeroed"), sem("valid_ready")
        m.recips, m.ctx_split, m.conv, m.maxima_taken = (
            sem("recips"), sem("ctx_split"), sem("conv"), sem("maxima_taken"))
        m.rows_masked, m.high, m.channel_mean = sem("rows_masked"), sem("high"), sem("channel_mean")
        m.sync_passed, m.pool_passed = sem("sync_passed"), sem("pool_passed")
        m.tokens_in, m.rows_in, m.xm_in = sem("tokens_in"), sem("rows_in"), sem("xm_in")
        m.out_rows_in, m.g_in = sem("out_rows_in"), sem("g_in")
        m.x1_in, m.y_stored = sems("x1_in", 2), sems("y_stored", 2)
        m.full, m.free = sems("full", 5), sems("free", 5)
        m.added = sems("added", 2)
        m.ab_in = [sems(f"ab_in{n}_head", 2) for n in range(4)]
        m.cd_in, m.max_in, m.tails_in = sems("cd_in", 2), sems("max_in", 2), sem("tails_in")
        m.out_stored = sems("out_stored", 2)

        setup(nc, m)
        short, full = ((path_memory(nc, m, plan), plan) for plan in (Plan(PACKED), Plan(T)))
        block = ctx.enter_context(nc.Block())

        @block.tensor
        def _(pe):
            fits = pe.value_load(m.most_valid[0:1, 0:1])
            with pe.If(fits < PACKED + 1):
                tensor_program(nc, pe, m, *short)
            with pe.Else():
                tensor_program(nc, pe, m, *full)

        @block.scalar
        def _(act):
            fits = act.value_load(m.most_valid[0:1, 0:1])
            with act.If(fits < PACKED + 1):
                scalar_program(nc, act, m, *short)
            with act.Else():
                scalar_program(nc, act, m, *full)

        @block.vector
        def _(dve):
            fits = dve.value_load(m.most_valid[0:1, 0:1])
            with dve.If(fits < PACKED + 1):
                vector_program(nc, dve, m, *short)
            with dve.Else():
                vector_program(nc, dve, m, *full)

        @block.gpsimd
        def _(pool):
            fits = pool.value_load(m.most_valid[0:1, 0:1])
            with pool.If(fits < PACKED + 1):
                gpsimd_program(nc, pool, m, *short)
            with pool.Else():
                gpsimd_program(nc, pool, m, *full)

        @block.sync
        def _(sp):
            fits = sp.value_load(m.most_valid[0:1, 0:1])
            with sp.If(fits < PACKED + 1):
                sync_program(nc, sp, m, *short)
            with sp.Else():
                sync_program(nc, sp, m, *full)


def kernel(x, cond_2048, L0_cond_Wq, L0_cond_Wo):
    import numpy as np
    import concourse.bacc as bacc
    from concourse.bass_utils import run_bass_kernel_spmd as run

    x, cond, wq, wo = (np.ascontiguousarray(a) for a in (x, cond_2048, L0_cond_Wq, L0_cond_Wo))
    arrays = {
        "xT": np.ascontiguousarray(x.transpose(0, 2, 1)).reshape(B * T, D),
        "x": x.reshape(B * D, T),
        "maskT": np.ascontiguousarray(cond.reshape(B * TT, P).T),
        "wqT": np.ascontiguousarray(wq.T),
        "woT": np.ascontiguousarray(wo.T),
        "wq": wq,
    }
    nc = bacc.Bacc("TRN2", target_bir_lowering=False, num_devices=1)
    args = [nc.dram_tensor(name, a.shape, F32, kind="ExternalInput").ap() for name, a in arrays.items()]
    out = nc.dram_tensor("out", [B * T, D], F32, kind="ExternalOutput").ap()
    cond_attn_conv(nc, *args, out)
    got = run(nc, [arrays], core_ids=[0]).results[0]["out"]
    return np.ascontiguousarray(np.asarray(got).reshape(B, T, D).transpose(0, 2, 1))
```
